# Optimizing a Trainium2 kernel written in Bass

```python
import numpy as np
import jax
import jax.numpy as jnp

def _softmax(x, axis=-1):
    return jax.nn.softmax(x, axis=axis)

def _gelu(x):
    return jax.nn.gelu(x, approximate=True)

def _silu(x):
    return jax.nn.silu(x)

def _sigmoid(x):
    return jax.nn.sigmoid(x)

def _layernorm(x, axis=-1, eps=1e-05):
    m = jnp.mean(x, axis=axis, keepdims=True)
    v = jnp.var(x, axis=axis, keepdims=True)
    return (x - m) / jnp.sqrt(v + eps)

def _scatter_add(tgt, idx, src, axis=0):
    return tgt.at[idx].add(src)

def _segment_sum(src, seg, n):
    return jax.ops.segment_sum(src, seg, n)
kernel_name = 'mk_seq_postln_d2_jaxref_r8_f00da6'

def setup_inputs(seed: int=0):
    np.random.seed(seed)
    _w = jnp.asarray

    def _L0_attn_setup():
        import jax, jax.numpy as jnp
        import numpy as np
        import math
        B, S, DM, H = (4, 512, 128, 16)
        HD = DM // H
        key = jax.random.key(seed)
        ks = jax.random.split(key, 5)

        def xavier(k, shape):
            bound = math.sqrt(6.0 / (shape[0] + shape[1]))
            return jax.random.uniform(k, shape, jnp.float32, -bound, bound)
        return {'x': jax.random.normal(ks[0], (B, S, DM), jnp.float32), 'Wq': xavier(ks[1], (DM, DM)), 'Wk': xavier(ks[2], (DM, DM)), 'Wv': xavier(ks[3], (DM, DM)), 'Wfc': xavier(ks[4], (DM, DM))}
    _L0_attn_in = _L0_attn_setup()

    def _L0_ffn_setup():
        import jax, jax.numpy as jnp
        import numpy as np
        DIM = 128
        HIDDEN = 384
        SCALE = 1.0 / 127.0

        def _dequant(w_int, dtype):
            return w_int.astype(dtype) * jnp.asarray(SCALE, dtype)
        key = jax.random.key(seed)
        k_x, k_g, k_u, k_d = jax.random.split(key, 4)
        x = jax.random.normal(k_x, (4, 256, DIM), dtype=jnp.float32)
        w_gate = jax.random.randint(k_g, (HIDDEN, DIM), -127, 128, dtype=jnp.int32)
        w_up = jax.random.randint(k_u, (HIDDEN, DIM), -127, 128, dtype=jnp.int32)
        w_down = jax.random.randint(k_d, (DIM, HIDDEN), -127, 128, dtype=jnp.int32)
        return {'x': x, 'w_gate': w_gate, 'w_up': w_up, 'w_down': w_down}
    _L0_ffn_in = _L0_ffn_setup()

    def _L1_attn_setup():
        import jax, jax.numpy as jnp
        import numpy as np
        NUM_BLOCKS = 8
        D = 128
        FF = 512
        B, S = (4, 512)
        EPS_ATTN = 1e-06
        EPS_LN = 1e-06

        def _ln(x, scale, bias):
            m = jnp.mean(x, axis=-1, keepdims=True)
            v = jnp.var(x, axis=-1, keepdims=True)
            return (x - m) * jax.lax.rsqrt(v + EPS_LN) * scale + bias

        def _forward(x, Wq, bq, Wk, bk, Wv, bv, Wo, bo, ln1_s, ln1_b, W1, b1, W2, b2, ln2_s, ln2_b):
            gelu = lambda t: jax.nn.gelu(t, approximate=True)
            fmap = lambda t: jax.nn.elu(t) + 1.0
            for i in range(NUM_BLOCKS):
                residual = x
                Q = fmap(x @ Wq[i] + bq[i])
                K = fmap(x @ Wk[i] + bk[i])
                value = x @ Wv[i] + bv[i]
                KV = jnp.einsum('nsh,nsh->nh', K, value)
                Ksum = jnp.sum(K, axis=1)
                Z = 1.0 / (Q * Ksum[:, None, :] + EPS_ATTN)
                V = Q * KV[:, None, :] * Z
                attn_out = gelu(V @ Wo[i] + bo[i])
                x = _ln(attn_out + residual, ln1_s[i], ln1_b[i])
                residual = x
                h = gelu(x @ W1[i] + b1[i])
                ff_out = gelu(h @ W2[i] + b2[i])
                x = _ln(ff_out + residual, ln2_s[i], ln2_b[i])
            return x
        key = jax.random.key(seed)
        ks = jax.random.split(key, 16)
        g = lambda k, shape, fan: jax.random.normal(k, shape, jnp.float32) * (1.0 / np.sqrt(fan))
        inp = {'x': jax.random.normal(ks[0], (B, S, D), jnp.float32), 'Wq': g(ks[1], (NUM_BLOCKS, D, D), D), 'bq': jnp.zeros((NUM_BLOCKS, D), jnp.float32), 'Wk': g(ks[2], (NUM_BLOCKS, D, D), D), 'bk': jnp.zeros((NUM_BLOCKS, D), jnp.float32), 'Wv': g(ks[3], (NUM_BLOCKS, D, D), D), 'bv': jnp.zeros((NUM_BLOCKS, D), jnp.float32), 'Wo': g(ks[4], (NUM_BLOCKS, D, D), D), 'bo': jnp.zeros((NUM_BLOCKS, D), jnp.float32), 'ln1_s': jnp.ones((NUM_BLOCKS, D), jnp.float32), 'ln1_b': jnp.zeros((NUM_BLOCKS, D), jnp.float32), 'W1': g(ks[5], (NUM_BLOCKS, D, FF), D), 'b1': jnp.zeros((NUM_BLOCKS, FF), jnp.float32), 'W2': g(ks[6], (NUM_BLOCKS, FF, D), FF), 'b2': jnp.zeros((NUM_BLOCKS, D), jnp.float32), 'ln2_s': jnp.ones((NUM_BLOCKS, D), jnp.float32), 'ln2_b': jnp.zeros((NUM_BLOCKS, D), jnp.float32)}
        return inp
    _L1_attn_in = _L1_attn_setup()

    def _L1_ffn_setup():
        import jax, jax.numpy as jnp
        import numpy as np
        B, S, D = (1, 256, 128)
        E, K, F = (64, 8, 96)
        SF = 96
        C = 64
        ROUTED_SCALE = 1.0

        def _moe_forward(x, router_w, w_gate, w_up, w_down, ws_gate_up, ws_down):
            T = x.shape[0]
            logits = x.astype(jnp.float32) @ router_w.T
            probs = jax.nn.softmax(logits, axis=-1)
            topk_w, topk_ids = jax.lax.top_k(probs, K)
            topk_w = topk_w / jnp.sum(topk_w, axis=-1, keepdims=True)
            topk_w = topk_w.astype(x.dtype)
            N = T * K
            flat_e = topk_ids.reshape(-1)
            flat_w = topk_w.reshape(-1)
            tok = jnp.arange(N) // K
            onehot = flat_e[:, None] == jnp.arange(E)[None, :]
            pos = jnp.cumsum(onehot, axis=0)[jnp.arange(N), flat_e] - 1
            valid = pos < C
            idx = jnp.where(valid, flat_e * C + pos, E * C)
            x_buf = jnp.zeros((E * C + 1, x.shape[1]), x.dtype).at[idx].set(x[tok])
            xb = x_buf[:E * C].reshape(E, C, -1)
            g = jnp.einsum('ecd,edf->ecf', xb, w_gate)
            u = jnp.einsum('ecd,edf->ecf', xb, w_up)
            h = jax.nn.silu(g) * u
            y = jnp.einsum('ecf,efd->ecd', h, w_down).reshape(E * C, -1)
            safe = jnp.where(valid, idx, 0)
            contrib = y[safe] * (flat_w * valid.astype(flat_w.dtype))[:, None]
            routed = jax.ops.segment_sum(contrib, tok, num_segments=T)
            routed = routed * ROUTED_SCALE
            gu = x @ ws_gate_up
            sg, su = (gu[:, :SF], gu[:, SF:])
            shared = jax.nn.silu(sg) * su @ ws_down
            return routed + shared
        key = jax.random.key(seed)
        ks = jax.random.split(key, 7)
        w = 0.02
        return {'hidden_states': jax.random.normal(ks[0], (B, S, D), jnp.float32), 'router_w': jax.random.normal(ks[1], (E, D), jnp.float32) * w, 'w_gate': jax.random.normal(ks[2], (E, D, F), jnp.float32) * w, 'w_up': jax.random.normal(ks[3], (E, D, F), jnp.float32) * w, 'w_down': jax.random.normal(ks[4], (E, F, D), jnp.float32) * w, 'ws_gate_up': jax.random.normal(ks[5], (D, 2 * SF), jnp.float32) * w, 'ws_down': jax.random.normal(ks[6], (SF, D), jnp.float32) * w}
    _L1_ffn_in = _L1_ffn_setup()
    _d = {'L0_attn_x': _L0_attn_in['x'], 'L0_attn_Wq': _L0_attn_in['Wq'], 'L0_attn_Wk': _L0_attn_in['Wk'], 'L0_attn_Wv': _L0_attn_in['Wv'], 'L0_attn_Wfc': _L0_attn_in['Wfc'], 'L0_ffn_w_gate': _L0_ffn_in['w_gate'], 'L0_ffn_w_up': _L0_ffn_in['w_up'], 'L0_ffn_w_down': _L0_ffn_in['w_down'], 'L1_attn_Wq': _L1_attn_in['Wq'], 'L1_attn_bq': _L1_attn_in['bq'], 'L1_attn_Wk': _L1_attn_in['Wk'], 'L1_attn_bk': _L1_attn_in['bk'], 'L1_attn_Wv': _L1_attn_in['Wv'], 'L1_attn_bv': _L1_attn_in['bv'], 'L1_attn_Wo': _L1_attn_in['Wo'], 'L1_attn_bo': _L1_attn_in['bo'], 'L1_attn_ln1_s': _L1_attn_in['ln1_s'], 'L1_attn_ln1_b': _L1_attn_in['ln1_b'], 'L1_attn_W1': _L1_attn_in['W1'], 'L1_attn_b1': _L1_attn_in['b1'], 'L1_attn_W2': _L1_attn_in['W2'], 'L1_attn_b2': _L1_attn_in['b2'], 'L1_attn_ln2_s': _L1_attn_in['ln2_s'], 'L1_attn_ln2_b': _L1_attn_in['ln2_b'], 'L1_ffn_router_w': _L1_ffn_in['router_w'], 'L1_ffn_w_gate': _L1_ffn_in['w_gate'], 'L1_ffn_w_up': _L1_ffn_in['w_up'], 'L1_ffn_w_down': _L1_ffn_in['w_down'], 'L1_ffn_ws_gate_up': _L1_ffn_in['ws_gate_up'], 'L1_ffn_ws_down': _L1_ffn_in['ws_down']}
    _x0 = _d['L0_attn_x']
    _d['L0_attn_x'] = jax.random.normal(jax.random.fold_in(jax.random.key(seed), 1), (8, 512, 128), dtype=_x0.dtype)
    del _x0
    return _d

def reference(L0_attn_x, L0_attn_Wq, L0_attn_Wk, L0_attn_Wv, L0_attn_Wfc, L0_ffn_w_gate, L0_ffn_w_up, L0_ffn_w_down, L1_attn_Wq, L1_attn_bq, L1_attn_Wk, L1_attn_bk, L1_attn_Wv, L1_attn_bv, L1_attn_Wo, L1_attn_bo, L1_attn_ln1_s, L1_attn_ln1_b, L1_attn_W1, L1_attn_b1, L1_attn_W2, L1_attn_b2, L1_attn_ln2_s, L1_attn_ln2_b, L1_ffn_router_w, L1_ffn_w_gate, L1_ffn_w_up, L1_ffn_w_down, L1_ffn_ws_gate_up, L1_ffn_ws_down):

    def _L0_attn_ref(x, Wq, Wk, Wv, Wfc):
        import jax, jax.numpy as jnp
        import numpy as np
        import math
        B, S, DM, H = (4, 512, 128, 16)
        HD = DM // H
        b, s, dm = x.shape
        h, hd = (H, dm // H)
        Q = (x @ Wq.T).reshape(b, s, h, hd)
        K = (x @ Wk.T).reshape(b, s, h, hd)
        V = (x @ Wv.T).reshape(b, s, h, hd)
        scores = jnp.einsum('bshd,bstd->bsht', Q, K) / math.sqrt(hd)
        attn = jax.nn.softmax(scores, axis=-1)
        out = jnp.einsum('bsht,bstd->bshd', attn, V).reshape(b, s, dm)
        return out @ Wfc.T

    def _L0_ffn_ref(x, w_gate, w_up, w_down):
        import jax, jax.numpy as jnp
        import numpy as np
        DIM = 128
        HIDDEN = 384
        SCALE = 1.0 / 127.0

        def _dequant(w_int, dtype):
            return w_int.astype(dtype) * jnp.asarray(SCALE, dtype)
        wg = _dequant(w_gate, x.dtype)
        wu = _dequant(w_up, x.dtype)
        wd = _dequant(w_down, x.dtype)
        gate = jnp.einsum('bsd,hd->bsh', x, wg)
        up = jnp.einsum('bsd,hd->bsh', x, wu)
        h = jax.nn.silu(gate) * up
        return jnp.einsum('bsh,dh->bsd', h, wd)

    def _L1_attn_ref(x, Wq, bq, Wk, bk, Wv, bv, Wo, bo, ln1_s, ln1_b, W1, b1, W2, b2, ln2_s, ln2_b):
        import jax, jax.numpy as jnp
        import numpy as np
        NUM_BLOCKS = 8
        D = 128
        FF = 512
        B, S = (4, 512)
        EPS_ATTN = 1e-06
        EPS_LN = 1e-06

        def _ln(x, scale, bias):
            m = jnp.mean(x, axis=-1, keepdims=True)
            v = jnp.var(x, axis=-1, keepdims=True)
            return (x - m) * jax.lax.rsqrt(v + EPS_LN) * scale + bias

        def _forward(x, Wq, bq, Wk, bk, Wv, bv, Wo, bo, ln1_s, ln1_b, W1, b1, W2, b2, ln2_s, ln2_b):
            gelu = lambda t: jax.nn.gelu(t, approximate=True)
            fmap = lambda t: jax.nn.elu(t) + 1.0
            for i in range(NUM_BLOCKS):
                residual = x
                Q = fmap(x @ Wq[i] + bq[i])
                K = fmap(x @ Wk[i] + bk[i])
                value = x @ Wv[i] + bv[i]
                KV = jnp.einsum('nsh,nsh->nh', K, value)
                Ksum = jnp.sum(K, axis=1)
                Z = 1.0 / (Q * Ksum[:, None, :] + EPS_ATTN)
                V = Q * KV[:, None, :] * Z
                attn_out = gelu(V @ Wo[i] + bo[i])
                x = _ln(attn_out + residual, ln1_s[i], ln1_b[i])
                residual = x
                h = gelu(x @ W1[i] + b1[i])
                ff_out = gelu(h @ W2[i] + b2[i])
                x = _ln(ff_out + residual, ln2_s[i], ln2_b[i])
            return x
        return _forward(x, Wq, bq, Wk, bk, Wv, bv, Wo, bo, ln1_s, ln1_b, W1, b1, W2, b2, ln2_s, ln2_b)

    def _L1_ffn_ref(hidden_states, router_w, w_gate, w_up, w_down, ws_gate_up, ws_down):
        import jax, jax.numpy as jnp
        import numpy as np
        B, S, D = (1, 256, 128)
        E, K, F = (64, 8, 96)
        SF = 96
        C = 64
        ROUTED_SCALE = 1.0

        def _moe_forward(x, router_w, w_gate, w_up, w_down, ws_gate_up, ws_down):
            T = x.shape[0]
            logits = x.astype(jnp.float32) @ router_w.T
            probs = jax.nn.softmax(logits, axis=-1)
            topk_w, topk_ids = jax.lax.top_k(probs, K)
            topk_w = topk_w / jnp.sum(topk_w, axis=-1, keepdims=True)
            topk_w = topk_w.astype(x.dtype)
            N = T * K
            flat_e = topk_ids.reshape(-1)
            flat_w = topk_w.reshape(-1)
            tok = jnp.arange(N) // K
            onehot = flat_e[:, None] == jnp.arange(E)[None, :]
            pos = jnp.cumsum(onehot, axis=0)[jnp.arange(N), flat_e] - 1
            valid = pos < C
            idx = jnp.where(valid, flat_e * C + pos, E * C)
            x_buf = jnp.zeros((E * C + 1, x.shape[1]), x.dtype).at[idx].set(x[tok])
            xb = x_buf[:E * C].reshape(E, C, -1)
            g = jnp.einsum('ecd,edf->ecf', xb, w_gate)
            u = jnp.einsum('ecd,edf->ecf', xb, w_up)
            h = jax.nn.silu(g) * u
            y = jnp.einsum('ecf,efd->ecd', h, w_down).reshape(E * C, -1)
            safe = jnp.where(valid, idx, 0)
            contrib = y[safe] * (flat_w * valid.astype(flat_w.dtype))[:, None]
            routed = jax.ops.segment_sum(contrib, tok, num_segments=T)
            routed = routed * ROUTED_SCALE
            gu = x @ ws_gate_up
            sg, su = (gu[:, :SF], gu[:, SF:])
            shared = jax.nn.silu(sg) * su @ ws_down
            return routed + shared
        b, s, d = hidden_states.shape
        x = hidden_states.reshape(-1, d)
        out = _moe_forward(x, router_w, w_gate, w_up, w_down, ws_gate_up, ws_down)
        return out.reshape(b, s, d)
    x = L0_attn_x
    x = _layernorm(x + _L0_attn_ref(x, L0_attn_Wq, L0_attn_Wk, L0_attn_Wv, L0_attn_Wfc), axis=-1)
    x = _layernorm(x + _L0_ffn_ref(x, L0_ffn_w_gate, L0_ffn_w_up, L0_ffn_w_down), axis=-1)
    x = _layernorm(x + _L1_attn_ref(x, L1_attn_Wq, L1_attn_bq, L1_attn_Wk, L1_attn_bk, L1_attn_Wv, L1_attn_bv, L1_attn_Wo, L1_attn_bo, L1_attn_ln1_s, L1_attn_ln1_b, L1_attn_W1, L1_attn_b1, L1_attn_W2, L1_attn_b2, L1_attn_ln2_s, L1_attn_ln2_b), axis=-1)
    x = _layernorm(x + _L1_ffn_ref(x, L1_ffn_router_w, L1_ffn_w_gate, L1_ffn_w_up, L1_ffn_w_down, L1_ffn_ws_gate_up, L1_ffn_ws_down), axis=-1)
    return x

_drawn_inputs = setup_inputs


def setup_inputs(seed=0):
    import zlib

    import numpy as np

    out = dict(_drawn_inputs(seed))
    spreads = {'L1_attn_bq': (0.0, 0.8),
     'L1_attn_bk': (0.0, 0.8),
     'L1_attn_bv': (0.0, 0.1),
     'L1_attn_bo': (0.0, 0.1),
     'L1_attn_ln1_s': (1.0, 0.2),
     'L1_attn_ln1_b': (0.0, 0.1),
     'L1_attn_b1': (0.0, 0.1),
     'L1_attn_b2': (0.0, 0.1),
     'L1_attn_ln2_s': (1.0, 0.2),
     'L1_attn_ln2_b': (0.0, 0.1)}
    factors = {'L1_attn_Wq': 8.0,
     'L1_ffn_router_w': 8.0,
     'L1_ffn_w_gate': 8.0,
     'L1_ffn_w_up': 8.0,
     'L1_ffn_w_down': 8.0,
     'L1_ffn_ws_gate_up': 8.0,
     'L1_ffn_ws_down': 8.0}
    for name, (base, spread) in spreads.items():
        noise = np.random.default_rng([zlib.crc32(name.encode()), seed]).standard_normal(out[name].shape)
        drawn = base * np.exp(spread * noise) if base else spread * noise
        out[name] = jnp.asarray(drawn.astype(out[name].dtype))
    for name, factor in factors.items():
        out[name] = (out[name] * factor).astype(out[name].dtype)
    return out
```

```python
from contextlib import ExitStack

import concourse.bass as bass
from concourse import mybir

F32 = mybir.dt.float32
BF16 = mybir.dt.bfloat16
I32 = mybir.dt.int32
U32 = mybir.dt.uint32
ALU = mybir.AluOpType
ACT = mybir.ActivationFunctionType
AX = mybir.AxisListType

P = 128
D = 128
TOKENS = 8 * 512
TILE = 128
NT = TOKENS // TILE
CH = 512
NC = TOKENS // CH
TPC = CH // TILE
HEADS, HD = 16, 8
HIDDEN, NJ = 384, 3
BLOCKS = 8
FF, NF = 512, 4
E, TOPK, CAP, FE = 64, 8, 64, 96
PAIRS = E // 2
ROW = D + 2 * E
DUMP = TOKENS * TOPK
EXP_LN_SET = "natural_log_exp_and_others"
GELU_SET = "gelu_apprx_tanh_and_others"
W1COLS = 3 * D + 3
O_F1 = D + 1
O_F2 = O_F1 + FF + NF + 2
O_LN2 = O_F2 + NF * D + 1
W2COLS = O_LN2 + 2


def lagged(k, u, lag, unroll=2):
    r = (u - lag) % unroll
    g = k + (u - lag - r) // unroll
    return g, g * unroll + r, r


def live(k, u, lag, n, unroll=2):
    return not isinstance(k, int) or 0 <= k * unroll + u - lag < n


def steps(eng, n, depth, body, unroll=2, ring=None, rolled=True):
    head = min(-(-(depth + (ring or unroll)) // unroll), n // unroll) if rolled else n // unroll
    for k in range(head):
        for u in range(unroll):
            body(k, u)
    if head < n // unroll:
        with eng.Fori(head, n // unroll) as k:
            for u in range(unroll):
                body(k, u)
    for s in range(n, n + depth):
        body(s // unroll, s % unroll)


def beyond(t, n):
    return not isinstance(t, int) or t >= n


class Shared:

    def __init__(self, nc, ctx):
        sb = lambda n, s, t=F32: ctx.enter_context(nc.sbuf_tensor(n, s, t))
        self.ps = [ctx.enter_context(nc.psum_tensor(f"bank{i}", [P, 512], F32)) for i in range(8)]
        self.ident = sb("ident", [P, P])
        self.tri, self.ones = sb("tri", [P, P], BF16), sb("ones", [P, P], BF16)
        self.parmask = sb("parmask", [P, 2])
        self.eps5, self.eps6, self.mhalf = sb("eps5", [P, TPC]), sb("eps6", [P, TPC]), sb("mhalf", [P, TPC])
        self.iota_p, self.iota_pf = sb("iota_p", [P, 1], I32), sb("iota_pf", [P, 1])
        self.iota_c, self.place_of = sb("iota_c", [P, CAP], I32), sb("place_of", [P, P], BF16)
        self.xt, self.xt0 = sb("xt", [P, TOKENS]), sb("xt0", [P, TOKENS])
        self.base = sb("base", [P, NT, D])
        self.zeros = sb("zeros", [P, 2048])
        self.rows = nc.dram_tensor("rows", [TOKENS, ROW], F32).ap()
        self.contrib = nc.dram_tensor("contrib", [DUMP, D], F32).ap()
        self.x_ready = ctx.enter_context(nc.semaphore("x_ready"))


def constants(nc, k, a):
    with ExitStack() as ctx:
        s_zero = ctx.enter_context(nc.semaphore("c_zero"))
        s_sel = ctx.enter_context(nc.semaphore("c_sel"))
        s_iota = ctx.enter_context(nc.semaphore("c_iota"))
        s_eps = ctx.enter_context(nc.semaphore("c_eps"))
        block = ctx.enter_context(nc.Block())

        @block.gpsimd
        def _(pool):
            pool.memset(k.ident[:], 0.0).then_inc(s_zero, 1)
            pool.memset(k.tri[:], 1.0).then_inc(s_zero, 1)
            pool.memset(k.ones[:], 1.0).then_inc(s_zero, 1)
            pool.wait_ge(s_zero, 3)
            pool.affine_select(out=k.ident[:], in_=k.ident[:], compare_op=ALU.not_equal, fill=1.0,
                               base=0, pattern=[[-1, P]], channel_multiplier=1).then_inc(s_sel, 1)
            pool.affine_select(out=k.tri[:], in_=k.tri[:], compare_op=ALU.is_gt, fill=0.0,
                               base=0, pattern=[[1, P]], channel_multiplier=-1).then_inc(s_sel, 1)
            pool.iota(k.iota_p[:], pattern=[[0, 1]], base=0, channel_multiplier=1).then_inc(s_iota, 1)
            pool.iota(k.iota_c[:], pattern=[[1, CAP]], base=0, channel_multiplier=0).then_inc(s_iota, 1)

        @block.vector
        def _(dve):
            dve.memset(k.eps5[:], 1e-5).then_inc(s_eps, 1)
            dve.memset(k.zeros[:], 0.0).then_inc(s_eps, 1)
            dve.memset(k.eps6[:], 1e-6).then_inc(s_eps, 1)
            dve.memset(k.mhalf[:], -0.5).then_inc(s_eps, 1)
            dve.wait_ge(s_iota, 2)
            dve.tensor_copy(k.place_of[:].rearrange("p (c q) -> p c q", q=2),
                            k.iota_c[:].unsqueeze(2).to_broadcast([P, CAP, 2])).then_inc(s_eps, 1)
            dve.wait_ge(s_sel, 2)
            dve.tensor_reduce(k.parmask[:], k.ident[:].rearrange("p (m q) -> p q m", q=2), AX.X, ALU.add).then_inc(s_eps, 1)
            dve.tensor_copy(k.iota_pf[:], k.iota_p[:]).then_inc(s_eps, 1)


def cleared_later(nc, ctx, prefix):
    made = []

    def clear():
        nc.clear_and_free_semaphores(made)
        nc.all_engine_barrier()
    ctx.callback(clear)

    def sem(name):
        made.append(nc.alloc_semaphore(name=prefix + name))
        return made[-1]
    return sem


def stage_a(nc, k, a):
    with ExitStack() as ctx:
        sb = lambda n, s, t=F32: ctx.enter_context(nc.sbuf_tensor("a_" + n, s, t))
        sem = cleared_later(nc, ctx, "a_")
        wqkv, wfc = sb("wqkv", [P, 3 * D]), sb("wfc", [P, D])
        x_in = sb("x_in", [P, 2, TILE])
        x_res = sb("x_res", [P, 2, D])
        qkv = sb("qkv", [P, 2, D])
        prod = sb("prod", [P, 2, HD, HEADS * HEADS])
        top = sb("top", [P, 2, HEADS])
        shifted = sb("shifted", [P, 2, 256])
        expd = sb("expd", [P, 2, 256])
        den, rden = sb("den", [P, 4, HEADS]), sb("rden", [P, 4, HEADS])
        pv = sb("pv", [P, 2, HEADS, D])
        pvh = sb("pvh", [P, 2, HEADS // 2, D])
        o_nat, o_t = sb("o_nat", [P, 2, D]), sb("o_t", [P, 2, TILE])
        y, st, mv, rstd, xn = sb("y", [P, 2, D]), sb("st", [P, 2, 6]), sb("mv", [P, 2, 2]), sb("rstd", [P, 2, 1]), sb("xn", [P, 2, D])
        ps = k.ps
        w_in = sem("w_in")
        x_here = [sem("x_here0"), sem("x_here1")]
        r_here = [sem("r_here0"), sem("r_here1")]
        (qkv_done, q_sb, prod_done, score_done, shift_done, exp_done, pvp_done, half_done, pv_done,
         norm_done, ot_done, ot_sb, fc_done, stat_done, rstd_done, xn_done, back_done, xt_done, dsem) = map(
            sem, "qkv_done q_sb prod_done score_done shift_done exp_done pvp_done half_done pv_done "
                 "norm_done ot_done ot_sb fc_done stat_done rstd_done xn_done back_done xt_done dsem".split())
        var, var_done = sb("var", [P, 2, 1]), sem("var_done")
        soft, topped, rden_done = sem("soft"), sem("topped"), sem("rden_done")
        block = ctx.enter_context(nc.Block())
        DEPTH = 9
        L_SC, L_PVP, L_PV, L_NORM, L_OT, L_FC, L_LN, L_XN, L_BACK = 1, 2, 3, 4, 5, 6, 7, 8, 9
        NDVE = 6

        @block.sync
        def _(sp):
            sp.dma_start(wqkv[:], a["wqkv"]).then_inc(w_in, 16)
            sp.dma_start(wfc[:], a["wfc"]).then_inc(w_in, 16)

            def step(kk, u):
                if live(kk, u, 0, NT):
                    g, t, r = lagged(kk, u, 0)
                    if beyond(t, 2):
                        sp.wait_ge(qkv_done, t - 1)
                    sp.dma_start(x_in[:, r, :], a["xt"][:, bass.ds(t * TILE, TILE)]).then_inc(x_here[r], 16)
                if live(kk, u, L_FC, NT):
                    g, t, r = lagged(kk, u, L_FC)
                    if beyond(t, 2):
                        sp.wait_ge(dsem, (t - 2) * 2 + 1)
                    sp.dma_start(x_res[:, r, :], a["x"][bass.ds(t * TILE, TILE), :]).then_inc(r_here[r], 16)
            steps(sp, NT, DEPTH, step)

        @block.tensor
        def _(pe):
            pe.wait_ge(w_in, 32)

            def step(kk, u):
                if live(kk, u, L_SC, NT):
                    g, t, r = lagged(kk, u, L_SC)
                    pe.wait_ge(prod_done, t + 1)
                    if beyond(t, 2):
                        pe.wait_ge(shift_done, t - 1)
                    for d in range(HD):
                        mm = pe.matmul(ps[2 + r][:, 0:256], k.ident[:], prod[:, r, d, :], start=d == 0, stop=d == HD - 1)
                    mm.then_inc(score_done, 1)
                if live(kk, u, 0, NT):
                    g, t, r = lagged(kk, u, 0)
                    pe.wait_ge(x_here[r], g * 16 + 16)
                    if beyond(t, 2):
                        pe.wait_ge(pvp_done, t - 1)
                    pe.matmul(ps[r][:, 0:3 * D], x_in[:, r, :], wqkv[:], start=True, stop=True).then_inc(qkv_done, 1)
                if live(kk, u, L_PV, NT):
                    g, t, r = lagged(kk, u, L_PV)
                    pe.wait_ge(half_done, t + 1)
                    if beyond(t, 1):
                        pe.wait_ge(norm_done, t)
                    for j in range(HEADS // 2):
                        mm = pe.matmul(ps[4][:, 0:D], k.ident[:], pvh[:, r, j, :], start=j == 0, stop=j == HEADS // 2 - 1)
                    mm.then_inc(pv_done, 1)
                if live(kk, u, L_OT, NT):
                    g, t, r = lagged(kk, u, L_OT)
                    pe.wait_ge(norm_done, t + 1)
                    if beyond(t, 1):
                        pe.wait_ge(ot_sb, t)
                    pe.transpose(ps[5][:, 0:TILE], o_nat[:, r, :], k.ident[:]).then_inc(ot_done, 1)
                if live(kk, u, L_FC, NT):
                    g, t, r = lagged(kk, u, L_FC)
                    pe.wait_ge(ot_sb, t + 1)
                    if beyond(t, 1):
                        pe.wait_ge(dsem, t * 2 - 1)
                    pe.matmul(ps[6][:, 0:D], o_t[:, r, :], wfc[:], start=True, stop=True).then_inc(fc_done, 1)
                if live(kk, u, L_BACK, NT):
                    g, t, r = lagged(kk, u, L_BACK)
                    pe.wait_ge(xn_done, t + 1)
                    if beyond(t, 1):
                        pe.wait_ge(xt_done, t)
                    pe.transpose(ps[7][:, 0:TILE], xn[:, r, :], k.ident[:]).then_inc(back_done, 1)
            steps(pe, NT, DEPTH, step)

        @block.scalar
        def _(act):
            def step(kk, u):
                if live(kk, u, 0, NT):
                    g, t, r = lagged(kk, u, 0)
                    act.wait_ge(qkv_done, t + 1)
                    if beyond(t, 2):
                        act.wait_ge(prod_done, t - 1)
                    act.activation(qkv[:, r, :], ps[r][:, 0:D], ACT.Copy).then_inc(q_sb, 1)
                if live(kk, u, L_SC, NT):
                    g, t, r = lagged(kk, u, L_SC)
                    act.wait_ge(shift_done, t + 1)
                    if beyond(t, 2):
                        act.wait_ge(soft, t - 1)
                    act.activation(expd[:, r, :], shifted[:, r, :], ACT.Exp, scale=HD ** -0.5).then_inc(exp_done, 1)
                if live(kk, u, L_OT, NT):
                    g, t, r = lagged(kk, u, L_OT)
                    act.wait_ge(ot_done, t + 1)
                    if beyond(t, 2):
                        act.wait_ge(fc_done, t - 1)
                    act.activation(o_t[:, r, :], ps[5][:, 0:TILE], ACT.Copy).then_inc(ot_sb, 1)
                if live(kk, u, L_BACK, NT):
                    g, t, r = lagged(kk, u, L_BACK)
                    act.wait_ge(back_done, t + 1)
                    act.activation(k.xt[:, bass.ds(t * TILE, TILE)], ps[7][:, 0:TILE], ACT.Copy).then_inc(xt_done, 1)
            steps(act, NT, DEPTH, step)

        @block.vector
        def _(dve):
            def step(kk, u):
                if live(kk, u, L_PVP, NT):
                    g, t, r = lagged(kk, u, L_PVP)
                    dve.wait_ge(exp_done, t + 1)
                    if beyond(t, 2):
                        dve.wait_ge(half_done, t - 1)
                    e = expd[:, r, :].rearrange("p (h t) -> p t h", h=HEADS)
                    v = ps[r][:, 2 * D:3 * D].rearrange("p (t d) -> p t d", d=HD)
                    dve.tensor_tensor(pv[:, r, :, :].rearrange("p t (h d) -> p t h d", d=HD),
                                      e.unsqueeze(3).to_broadcast([P, HEADS, HEADS, HD]),
                                      v.unsqueeze(2).to_broadcast([P, HEADS, HEADS, HD]), ALU.mult).then_inc(pvp_done, 1)
                    if beyond(t, 2):
                        dve.wait_ge(rden_done, t - 1)
                    dve.tensor_reduce(den[:, r, :], expd[:, r, :].rearrange("p (h t) -> p h t", h=HEADS),
                                      AX.X, ALU.add).then_inc(soft, 1)
                if live(kk, u, L_SC, NT):
                    g, t, r = lagged(kk, u, L_SC)
                    dve.wait_ge(score_done, t + 1)
                    sc = ps[2 + r][:, 0:256].rearrange("p (h t) -> p h t", h=HEADS)
                    dve.tensor_reduce(top[:, r, :], sc, AX.X, ALU.max).then_inc(topped, 1)
                if live(kk, u, L_NORM, NT):
                    g, t, r = lagged(kk, u, L_NORM)
                    dve.wait_ge(pv_done, t + 1)
                    dve.wait_ge(rden_done, t + 1)
                    if beyond(t, 2):
                        dve.wait_ge(ot_done, t - 1)
                    dve.tensor_tensor(o_nat[:, r, :].rearrange("p (h d) -> p h d", d=HD),
                                      ps[4][:, 0:D].rearrange("p (h d) -> p h d", d=HD),
                                      rden[:, r, :].unsqueeze(2).to_broadcast([P, HEADS, HD]), ALU.mult).then_inc(norm_done, 1)
                if live(kk, u, L_PVP, NT):
                    g, t, r = lagged(kk, u, L_PVP)
                    dve.wait_ge(soft, t + 1)
                    if beyond(t, 2):
                        dve.wait_ge(norm_done, t - 1)
                    dve.reciprocal(rden[:, r, :], den[:, r, :]).then_inc(rden_done, 1)
                if live(kk, u, L_SC, NT):
                    g, t, r = lagged(kk, u, L_SC)
                    dve.wait_ge(topped, t + 1)
                    if beyond(t, 2):
                        dve.wait_ge(exp_done, t - 1)
                    sc = ps[2 + r][:, 0:256].rearrange("p (h t) -> p h t", h=HEADS)
                    dve.tensor_tensor(shifted[:, r, :].rearrange("p (h t) -> p h t", h=HEADS), sc,
                                      top[:, r, :].unsqueeze(2).to_broadcast([P, HEADS, HEADS]), ALU.subtract).then_inc(shift_done, 1)
                if live(kk, u, L_LN, NT):
                    g, t, r = lagged(kk, u, L_LN)
                    dve.wait_ge(fc_done, t + 1)
                    dve.wait_ge(r_here[r], g * 16 + 16)
                    if beyond(t, 2):
                        dve.wait_ge(xn_done, t - 1)
                    dve.tensor_tensor(y[:, r, :], ps[6][:, 0:D], x_res[:, r, :], ALU.add).then_inc(dsem, 1)
                    dve.wait_ge(dsem, t * 2 + 1)
                    dve.bn_stats(st[:, r, :], y[:, r, :]).then_inc(dsem, 1)
                if live(kk, u, L_XN, NT):
                    g, t, r = lagged(kk, u, L_XN)
                    dve.wait_ge(rstd_done, t + 1)
                    if beyond(t, 2):
                        dve.wait_ge(back_done, t - 1)
                    if live(kk, u, L_LN, NT):
                        dve.wait_ge(dsem, lagged(kk, u, L_LN)[1] * 2 + 2)
                    dve.tensor_scalar(xn[:, r, :], y[:, r, :], mv[:, r, 0:1], rstd[:, r, :], ALU.subtract, ALU.mult).then_inc(xn_done, 1)
                if live(kk, u, L_LN, NT):
                    g, t, r = lagged(kk, u, L_LN)
                    if not live(kk, u, L_XN, NT):
                        dve.wait_ge(dsem, t * 2 + 2)
                    dve.bn_aggr(mv[:, r, :], st[:, r, :]).then_inc(stat_done, 1)
                if live(kk, u, 0, NT):
                    g, t, r = lagged(kk, u, 0)
                    dve.wait_ge(q_sb, t + 1)
                    if beyond(t, 2):
                        dve.wait_ge(score_done, t - 1)
                    q = qkv[:, r, :].rearrange("p (h d) -> p d h", d=HD)
                    kx = ps[r][:, D:2 * D].rearrange("p (t d) -> p d t", d=HD)
                    dve.tensor_tensor(prod[:, r, :, :].rearrange("p d (h t) -> p d h t", h=HEADS),
                                      q.unsqueeze(3).to_broadcast([P, HD, HEADS, HEADS]),
                                      kx.unsqueeze(2).to_broadcast([P, HD, HEADS, HEADS]), ALU.mult).then_inc(prod_done, 1)
            steps(dve, NT, DEPTH, step)

        @block.gpsimd
        def _(pool):
            def step(kk, u):
                if live(kk, u, L_PVP, NT):
                    g, t, r = lagged(kk, u, L_PVP)
                    pool.wait_ge(pvp_done, t + 1)
                    if beyond(t, 2):
                        pool.wait_ge(pv_done, t - 1)
                    h = HEADS // 2
                    pool.tensor_tensor(pvh[:, r, :, :], pv[:, r, 0:h, :], pv[:, r, h:2 * h, :], ALU.add).then_inc(half_done, 1)
                if live(kk, u, L_LN, NT):
                    g, t, r = lagged(kk, u, L_LN)
                    pool.wait_ge(stat_done, t + 1)
                    if beyond(t, 2):
                        pool.wait_ge(xn_done, t - 1)
                    pool.tensor_tensor(var[:, r, :], mv[:, r, 1:2], k.eps5[:, 0:1], ALU.add).then_inc(var_done, 1)
                    pool.wait_ge(var_done, t + 1)
                    pool.tensor_tensor(rstd[:, r, :], var[:, r, :], k.mhalf[:, 0:1], ALU.pow).then_inc(rstd_done, 1)
            steps(pool, NT, DEPTH, step)



class Norm:

    def __init__(self, nc, ctx, sem, name, fwd_bank, back_bank, eps, xn=None, ring=2):
        sb = lambda n, s: ctx.enter_context(nc.sbuf_tensor(f"{name}_{n}", s, F32))
        self.fwd, self.back, self.eps, self.ring = fwd_bank, back_bank, eps, ring
        self.mark, self.y = sb("mark", [P, 1]), sb("y", [P, 2, CH])
        self.st, self.mv = sb("st", [P, TPC, 6]), sb("mv", [P, TPC, 2])
        self.var, self.rstd = sb("var", [P, TPC]), sb("rstd", [P, 2, TPC])
        self.xn = sb("xn", [P, 2, TPC, D]) if xn is None else xn
        self.y_ready, self.fwd_done, self.stat_done, self.aggr_done, self.var_done, self.rstd_done, \
            self.xn_done, self.back_done = (sem(f"{name[2:]}_{n}") for n in (
                "y_ready", "fwd_done", "stat_done", "aggr_done", "var_done", "rstd_done", "xn_done", "back_done"))


def wait_older(eng, sem, n, ago):
    if beyond(n, ago):
        eng.wait_ge(sem, n - ago + 1)


def norm_fwd(pe, k, L, n, c):
    pe.wait_ge(L.y_ready, n + 1)
    wait_older(pe, L.xn_done, n, 1)
    for j in range(TPC):
        mm = pe.transpose(L.fwd[:, j * D:(j + 1) * D], L.y[:, c % 2, j * D:(j + 1) * D], k.ident[:])
    mm.then_inc(L.fwd_done, 1)


def norm_stats(dve, k, L, n, c):
    dve.wait_ge(L.fwd_done, n + 1)
    for j in range(TPC):
        st = dve.bn_stats(L.st[:, j, :], L.fwd[:, j * D:(j + 1) * D])
    st.then_inc(L.stat_done, 1)
    dve.wait_ge(L.stat_done, n + 1)
    dve.tensor_copy(L.mark[:], L.st[:, 0, 0:1])
    for j in range(TPC):
        ag = dve.bn_aggr(L.mv[:, j, :], L.st[:, j, :])
    ag.then_inc(L.aggr_done, 1)


def norm_rstd(pool, k, L, n, c):
    pool.wait_ge(L.aggr_done, n + 1)
    pool.tensor_tensor(L.var[:], L.mv[:, :, 1], L.eps[:], ALU.add).then_inc(L.var_done, 1)
    pool.wait_ge(L.var_done, n + 1)
    pool.tensor_tensor(L.rstd[:, c % 2, :], L.var[:], k.mhalf[:], ALU.pow).then_inc(L.rstd_done, 1)


def norm_apply(dve, k, L, n, c):
    dve.wait_ge(L.rstd_done, n + 1)
    wait_older(dve, L.back_done, n, L.ring)
    for j in range(TPC):
        ts = dve.tensor_scalar(L.xn[:, c % L.ring, j, :], L.fwd[:, j * D:(j + 1) * D], L.mv[:, j, 0:1],
                               L.rstd[:, c % 2, j:j + 1], ALU.subtract, ALU.mult)
    ts.then_inc(L.xn_done, 1)


def norm_back(pe, k, L, n, c):
    pe.wait_ge(L.xn_done, n + 1)
    for j in range(TPC):
        mm = pe.transpose(L.back[:, j * D:(j + 1) * D], L.xn[:, c % L.ring, j, :], k.ident[:])
    mm.then_inc(L.back_done, 1)


def stage_b(nc, k, a):
    with ExitStack() as ctx:
        sb = lambda n, s, t=F32: ctx.enter_context(nc.sbuf_tensor("b_" + n, s, t))
        sem = cleared_later(nc, ctx, "b_")
        wint = sb("wint", [P, 3 * HIDDEN], I32)
        w = sb("w", [P, 3 * HIDDEN])
        sg, h = sb("sg", [P, 2, CH]), sb("h", [P, 2, NJ, CH])
        w_in, w_done = sem("w_in"), sem("w_done")
        gate_done, up_done, silu_done, h_done, down_done = map(sem, "gate_done up_done silu_done h_done down_done".split())
        copied = sem("copied")
        ps = k.ps
        L = Norm(nc, ctx, sem, "b_ln", ps[5], ps[6], k.eps5)
        out_done = k.x_ready
        block = ctx.enter_context(nc.Block())
        DEPTH = 4
        at = lambda c: slice(c * CH, (c + 1) * CH)

        @block.sync
        def _(sp):
            sp.dma_start(wint[:], a["wffn"]).then_inc(w_in, 16)

        @block.tensor
        def _(pe):
            pe.wait_ge(w_done, 1)
            for s in range(NC + DEPTH):
                if s < NC:
                    for j in range(NJ):
                        m = NJ * s + j
                        if m >= 2:
                            pe.wait_ge(silu_done, m - 1)
                        pe.matmul(ps[m % 2][:], w[:, j * P:(j + 1) * P], k.xt[:, at(s)], start=True, stop=True).then_inc(gate_done, 1)
                        if m >= 2:
                            pe.wait_ge(h_done, m - 1)
                        pe.matmul(ps[2 + m % 2][:], w[:, HIDDEN + j * P:HIDDEN + (j + 1) * P], k.xt[:, at(s)],
                                  start=True, stop=True).then_inc(up_done, 1)
                if 0 <= s - 2 < NC:
                    norm_fwd(pe, k, L, s - 2, s - 2)
                if 0 <= s - 1 < NC:
                    c = s - 1
                    if c >= 1:
                        pe.wait_ge(L.y_ready, c)
                    for j in range(NJ):
                        pe.wait_ge(h_done, NJ * c + j + 1)
                        mm = pe.matmul(ps[4][:], w[:, 2 * HIDDEN + j * P:2 * HIDDEN + (j + 1) * P], h[:, c % 2, j, :],
                                       start=j == 0, stop=j == NJ - 1)
                    mm.then_inc(down_done, 1)
                if 0 <= s - 3 < NC:
                    wait_older(pe, out_done, s - 3, 1)
                    norm_back(pe, k, L, s - 3, s - 3)

        @block.scalar
        def _(act):
            for s in range(NC + DEPTH):
                if s < NC:
                    for j in range(NJ):
                        m = NJ * s + j
                        act.wait_ge(gate_done, m + 1)
                        if m >= 2:
                            act.wait_ge(h_done, m - 1)
                        act.activation(sg[:, m % 2, :], ps[m % 2][:], ACT.Silu).then_inc(silu_done, 1)
                if 0 <= s - 3 < NC:
                    c = s - 3
                    act.wait_ge(L.back_done, c + 1)
                    act.activation(k.xt[:, at(c)], L.back[:], ACT.Copy).then_inc(out_done, 1)

        @block.vector
        def _(dve):
            dve.wait_ge(w_in, 16)
            dve.tensor_scalar(w[:], wint[:], 1.0 / 127.0, None, ALU.mult).then_inc(w_done, 1)
            for s in range(NC + DEPTH):
                if 0 <= s - 3 < NC:
                    norm_apply(dve, k, L, s - 3, s - 3)
                if s < NC:
                    for j in range(NJ):
                        m = NJ * s + j
                        dve.wait_ge(silu_done, m + 1)
                        dve.wait_ge(up_done, m + 1)
                        if s >= 2:
                            dve.wait_ge(down_done, s - 1)
                        dve.tensor_tensor(h[:, s % 2, j, :], sg[:, m % 2, :], ps[2 + m % 2][:], ALU.mult).then_inc(h_done, 1)
                if 0 <= s - 2 < NC:
                    norm_stats(dve, k, L, s - 2, s - 2)
                if 0 <= s - 1 < NC:
                    c = s - 1
                    dve.wait_ge(down_done, c + 1)
                    if c >= 2:
                        dve.wait_ge(L.fwd_done, c - 1)
                    dve.tensor_tensor(L.y[:, c % 2, :], ps[4][:], k.xt[:, at(c)], ALU.add).then_inc(L.y_ready, 1)

        @block.gpsimd
        def _(pool):
            for s in range(NC + DEPTH):
                if 0 <= s - 2 < NC:
                    norm_rstd(pool, k, L, s - 2, s - 2)
                if 0 <= s - 4 < NC:
                    c = s - 4
                    pool.wait_ge(out_done, c + 1)
                    pool.tensor_copy(k.xt0[:, at(c)], k.xt[:, at(c)]).then_inc(copied, 1)


def stage_c(nc, k, a):
    N = BLOCKS * NC
    with ExitStack() as ctx:
        sb = lambda n, s, t=F32: ctx.enter_context(nc.sbuf_tensor("c_" + n, s, t))
        sem = cleared_later(nc, ctx, "c_")
        wqkv, wo = sb("wqkv", [P, W1COLS]), sb("wo", [P, D + 1])
        wf1, wf2 = sb("wf1", [P, FF + NF + 2]), sb("wf2", [P, NF * D + 1])
        ln2 = sb("ln2", [P, 2])
        b1p = sb("b1p", [P, 2])
        eq, ek, tq = sb("eq", [P, CH]), sb("ek", [P, CH]), sb("tq", [P, CH])
        qf, kf, kv = sb("qf", [P, 2, CH]), sb("kf", [P, CH]), sb("kv", [P, CH])
        ksum, kvsum = sb("ksum", [P, NC]), sb("kvsum", [P, NC])
        lz, z, qz = sb("lz", [P, CH]), sb("z", [P, CH]), sb("qz", [P, 2, CH])
        wo_kv = sb("wo_kv", [P, 2, D])
        g1, g2, h = sb("g1", [P, CH]), sb("g2", [P, CH]), sb("h", [P, 2, NF, CH])
        wqkv_in, wo_in, wf1_in, wf2_in, ln2_in, cleared = map(sem, "wqkv_in wo_in wf1_in wf2_in ln2_in cleared".split())
        (b1p_done, q_done, k_done, v_done, eq_done, ek_done, tq_done, eqmin_done, ekmin_done, qf_done, kf_done, kv_done,
         lz_done, z_done, qz_done, wokv_done, wo_done, g1_done, x1_done, hp_done, hg_done, w2_done, g2_done) = map(
            sem, "b1p_done q_done k_done v_done eq_done ek_done tq_done eqmin_done ekmin_done qf_done kf_done kv_done "
                 "lz_done z_done qz_done wokv_done wo_done g1_done x1_done hp_done hg_done w2_done g2_done".split())
        x_ready = k.x_ready
        contrib = k.contrib.rearrange("(p r) d -> p (r d)", p=P)
        b_q, b_k, b_v, b_g, b_h, b_fwd, b_back = k.ps[0], k.ps[1], k.ps[2], k.ps[3], k.ps[4:6], k.ps[6], k.ps[7]
        L1 = Norm(nc, ctx, sem, "c_ln1", b_fwd, b_back, k.eps6)
        L2 = Norm(nc, ctx, sem, "c_ln2", b_fwd, b_back, k.eps6)
        block = ctx.enter_context(nc.Block())
        at = lambda c: slice(c * CH, (c + 1) * CH)
        A_WO, A_N1, A_W2, A_N2 = 1, 2, 3, 4
        DEPTH = A_N2

        def done(eng, sem, kk, u, lag, per=1):
            if live(kk, u, lag, N, NC):
                eng.wait_ge(sem, (lagged(kk, u, lag, NC)[1] + 1) * per)

        def items(eng, body):
            steps(eng, N, DEPTH, body, NC, ring=2)

        @block.sync
        def _(sp):
            def load(to, w, g, cols, sem):
                sp.dma_start(to[:], w[bass.ds(g * P, P), cols]).then_inc(sem, 16)

            def body(kk):
                first = isinstance(kk, int) and kk == 0
                for to, w, cols, here, used, per in (
                        (wqkv, a["w1"], slice(0, W1COLS), wqkv_in, kv_done, 1),
                        (wo, a["w2"], slice(0, D + 1), wo_in, g1_done, 1),
                        (wf1, a["w2"], slice(O_F1, O_F2), wf1_in, hg_done, NF),
                        (wf2, a["w2"], slice(O_F2, O_LN2), wf2_in, g2_done, 1)):
                    if not first:
                        sp.wait_ge(used, kk * (NC * per))
                    load(to, w, kk, cols, here)
                if not first:
                    sp.wait_ge(x_ready, kk * NC + NC)
                load(ln2, a["w2"], kk, slice(O_LN2, W2COLS), ln2_in)
                for i in range(2):
                    sp.dma_start(contrib[:, bass.ds(kk * 4096 + i * 2048, 2048)], k.zeros[:]).then_inc(cleared, 16)
            body(0)
            with sp.Fori(1, BLOCKS) as kk:
                body(kk)
            sp.wait_ge(cleared, BLOCKS * 32)

        @block.tensor
        def _(pe):
            def step(kk, u):
                if live(kk, u, A_N1, N, NC):
                    g, n, c = lagged(kk, u, A_N1, NC)
                    done(pe, L2.xn_done, kk, u, A_N2 + 1)
                    norm_fwd(pe, k, L1, n, c)
                if live(kk, u, 0, N, NC):
                    g, n, c = lagged(kk, u, 0, NC)
                    if c == 0:
                        pe.wait_ge(wqkv_in, g * 16 + 16)
                    pe.wait_ge(x_ready, n + 1)
                    done(pe, tq_done, kk, u, 1)
                    pe.matmul(b_q[:], wqkv[:, 0:D], k.xt[:, at(c)], start=True, stop=True).then_inc(q_done, 1)
                    done(pe, kf_done, kk, u, 1)
                    pe.matmul(b_k[:], wqkv[:, D:2 * D], k.xt[:, at(c)], start=True, stop=True).then_inc(k_done, 1)
                    done(pe, kv_done, kk, u, 1)
                    pe.matmul(b_v[:], wqkv[:, 2 * D:3 * D], k.xt[:, at(c)], start=True, stop=True).then_inc(v_done, 1)
                if live(kk, u, A_W2, N, NC):
                    g, n, c = lagged(kk, u, A_W2, NC)
                    if c == 0:
                        pe.wait_ge(wf2_in, g * 16 + 16)
                    done(pe, g1_done, kk, u, A_WO + 1)
                    for j in range(NF):
                        pe.wait_ge(hg_done, n * NF + j + 1)
                        mm = pe.matmul(b_g[:], wf2[:, j * D:(j + 1) * D], h[:, c % 2, j, :], start=j == 0, stop=j == NF - 1)
                    mm.then_inc(w2_done, 1)
                if live(kk, u, A_N1, N, NC):
                    g, n, c = lagged(kk, u, A_N1, NC)
                    if live(kk, u, A_N2 + 1, N, NC):
                        pe.wait_ge(x_ready, lagged(kk, u, A_N2 + 1, NC)[1] + NC + 1)
                    norm_back(pe, k, L1, n, c)
                if live(kk, u, A_N2, N, NC):
                    g, n, c = lagged(kk, u, A_N2, NC)
                    done(pe, L1.xn_done, kk, u, A_N1)
                    norm_fwd(pe, k, L2, n, c)
                if live(kk, u, A_WO, N, NC):
                    g, n, c = lagged(kk, u, A_WO, NC)
                    pe.wait_ge(wokv_done, n + 1)
                    pe.wait_ge(qz_done, n + 1)
                    done(pe, g2_done, kk, u, A_W2)
                    pe.matmul(b_g[:], wo_kv[:, c % 2, :], qz[:, c % 2, :], start=True, stop=True).then_inc(wo_done, 1)
                if live(kk, u, A_N1, N, NC):
                    g, n, c = lagged(kk, u, A_N1, NC)
                    if c == 0:
                        pe.wait_ge(wf1_in, g * 16 + 16)
                    pe.wait_ge(x1_done, n + 1)
                    for j in range(NF):
                        if j >= 2:
                            pe.wait_ge(hg_done, n * NF + j - 1)
                        elif beyond(n, 1):
                            pe.wait_ge(hg_done, n * NF + j - 1)
                        pe.matmul(b_h[j % 2][:], wf1[:, j * P:(j + 1) * P], k.xt[:, at(c)], start=True, stop=True).then_inc(hp_done, 1)
                if live(kk, u, A_N2, N, NC):
                    g, n, c = lagged(kk, u, A_N2, NC)
                    done(pe, x1_done, kk, u, A_N1)
                    if not live(kk, u, A_N1, N, NC):
                        pe.wait_ge(x_ready, n + NC)
                    norm_back(pe, k, L2, n, c)
            items(pe, step)

        @block.scalar
        def _(act):
            def step(kk, u):
                act.preload_act_table_set(EXP_LN_SET)
                if live(kk, u, A_WO, N, NC):
                    g, n, c = lagged(kk, u, A_WO, NC)
                    act.wait_ge(kf_done, n + 1)
                    act.wait_ge(qf_done, n + 1)
                    act.activation(lz[:], qf[:, c % 2, :], ACT.Ln, bias=k.eps6[:, 0:1], scale=ksum[:, c:c + 1]).then_inc(lz_done, 1)
                    act.wait_ge(lz_done, n + 1)
                    done(act, qz_done, kk, u, A_WO + 1)
                    act.activation(z[:], lz[:], ACT.Exp, scale=-1.0).then_inc(z_done, 1)
                if live(kk, u, 0, N, NC):
                    g, n, c = lagged(kk, u, 0, NC)
                    act.wait_ge(q_done, n + 1)
                    done(act, qf_done, kk, u, 1)
                    act.activation(eq[:], b_q[:], ACT.Exp, bias=wqkv[:, 3 * D:3 * D + 1]).then_inc(eq_done, 1)
                    if c == 0:
                        act.wait_ge(b1p_done, g + 1)
                    act.activation(tq[:], b_q[:], ACT.Identity, bias=b1p[:, 0:1]).then_inc(tq_done, 1)
                    act.wait_ge(k_done, n + 1)
                    done(act, kf_done, kk, u, 1)
                    act.activation(ek[:], b_k[:], ACT.Exp, bias=wqkv[:, 3 * D + 1:3 * D + 2]).then_inc(ek_done, 1)
                act.preload_act_table_set(GELU_SET)
                if live(kk, u, A_W2, N, NC):
                    g, n, c = lagged(kk, u, A_W2, NC)
                    act.wait_ge(w2_done, n + 1)
                    done(act, L2.y_ready, kk, u, A_W2 + 1)
                    act.activation(g2[:], b_g[:], ACT.Gelu_apprx_tanh, bias=wf2[:, NF * D:NF * D + 1]).then_inc(g2_done, 1)
                if live(kk, u, A_N1, N, NC):
                    g, n, c = lagged(kk, u, A_N1, NC)
                    act.wait_ge(L1.back_done, n + 1)
                    if c == 0:
                        act.wait_ge(wf1_in, g * 16 + 16)
                    act.activation(k.xt[:, at(c)], b_back[:], ACT.Identity, bias=wf1[:, FF + NF + 1:FF + NF + 2],
                                   scale=wf1[:, FF + NF:FF + NF + 1]).then_inc(x1_done, 1)
                if live(kk, u, A_WO, N, NC):
                    g, n, c = lagged(kk, u, A_WO, NC)
                    act.wait_ge(wo_done, n + 1)
                    done(act, L1.y_ready, kk, u, A_WO + 1)
                    act.activation(g1[:], b_g[:], ACT.Gelu_apprx_tanh, bias=wo[:, D:D + 1]).then_inc(g1_done, 1)
                if live(kk, u, A_N1, N, NC):
                    g, n, c = lagged(kk, u, A_N1, NC)
                    done(act, w2_done, kk, u, A_N1 + 2)
                    for j in range(NF):
                        act.wait_ge(hp_done, n * NF + j + 1)
                        act.activation(h[:, c % 2, j, :], b_h[j % 2][:], ACT.Gelu_apprx_tanh, bias=wf1[:, FF + j:FF + j + 1]).then_inc(hg_done, 1)
                if live(kk, u, A_N2, N, NC):
                    g, n, c = lagged(kk, u, A_N2, NC)
                    if c == 0:
                        act.wait_ge(ln2_in, g * 16 + 16)
                    act.wait_ge(L2.back_done, n + 1)
                    act.activation(k.xt[:, at(c)], b_back[:], ACT.Identity, bias=ln2[:, 1:2], scale=ln2[:, 0:1]).then_inc(x_ready, 1)
            items(act, step)

        @block.vector
        def _(dve):
            def step(kk, u):
                if live(kk, u, A_WO, N, NC):
                    g, n, c = lagged(kk, u, A_WO, NC)
                    if c == 0:
                        dve.wait_ge(wo_in, g * 16 + 16)
                    dve.wait_ge(kv_done, n + 1)
                    done(dve, wo_done, kk, u, A_WO + 2)
                    dve.tensor_scalar(wo_kv[:, c % 2, :], wo[:, 0:D], kvsum[:, c:c + 1], None, ALU.mult).then_inc(wokv_done, 1)
                if live(kk, u, A_N1, N, NC):
                    g, n, c = lagged(kk, u, A_N1, NC)
                    norm_stats(dve, k, L1, n, c)
                    norm_apply(dve, k, L1, n, c)
                if live(kk, u, 0, N, NC):
                    g, n, c = lagged(kk, u, 0, NC)
                    if c == 0:
                        dve.wait_ge(wqkv_in, g * 16 + 16)
                        dve.tensor_scalar(b1p[:], wqkv[:, 3 * D:3 * D + 2], 1.0, None, ALU.add).then_inc(b1p_done, 1)
                    dve.wait_ge(eq_done, n + 1)
                    dve.tensor_scalar(eq[:], eq[:], 1.0, -1.0, ALU.min, ALU.add).then_inc(eqmin_done, 1)
                    dve.wait_ge(eqmin_done, n + 1)
                    dve.wait_ge(tq_done, n + 1)
                    done(dve, qz_done, kk, u, 2)
                    dve.scalar_tensor_tensor(qf[:, c % 2, :], eq[:], 1.0, tq[:], ALU.add, ALU.max).then_inc(qf_done, 1)
                    dve.wait_ge(ek_done, n + 1)
                    dve.tensor_scalar(ek[:], ek[:], 1.0, None, ALU.min).then_inc(ekmin_done, 1)
                    dve.wait_ge(ekmin_done, n + 1)
                    dve.scalar_tensor_tensor(kf[:], b_k[:], b1p[:, 1:2], ek[:], ALU.add, ALU.max,
                                             accum_out=ksum[:, c:c + 1]).then_inc(kf_done, 1)
                    dve.wait_ge(kf_done, n + 1)
                    dve.wait_ge(v_done, n + 1)
                    dve.scalar_tensor_tensor(kv[:], b_v[:], wqkv[:, 3 * D + 2:3 * D + 3], kf[:], ALU.add, ALU.mult,
                                             accum_out=kvsum[:, c:c + 1]).then_inc(kv_done, 1)
                if live(kk, u, A_N2, N, NC):
                    g, n, c = lagged(kk, u, A_N2, NC)
                    norm_stats(dve, k, L2, n, c)
                    norm_apply(dve, k, L2, n, c)
            items(dve, step)

        @block.gpsimd
        def _(pool):
            def step(kk, u):
                if live(kk, u, A_N1, N, NC):
                    g, n, c = lagged(kk, u, A_N1, NC)
                    norm_rstd(pool, k, L1, n, c)
                if live(kk, u, A_WO, N, NC):
                    g, n, c = lagged(kk, u, A_WO, NC)
                    pool.wait_ge(z_done, n + 1)
                    done(pool, wo_done, kk, u, A_WO + 2)
                    pool.tensor_tensor(qz[:, c % 2, :], qf[:, c % 2, :], z[:], ALU.mult).then_inc(qz_done, 1)
                if live(kk, u, A_W2, N, NC):
                    g, n, c = lagged(kk, u, A_W2, NC)
                    pool.wait_ge(g2_done, n + 1)
                    done(pool, L2.fwd_done, kk, u, A_W2 + 2)
                    pool.tensor_tensor(L2.y[:, c % 2, :], g2[:], k.xt[:, at(c)], ALU.add).then_inc(L2.y_ready, 1)
                if live(kk, u, A_N2, N, NC):
                    g, n, c = lagged(kk, u, A_N2, NC)
                    norm_rstd(pool, k, L2, n, c)
                if live(kk, u, A_WO, N, NC):
                    g, n, c = lagged(kk, u, A_WO, NC)
                    pool.wait_ge(g1_done, n + 1)
                    done(pool, L1.fwd_done, kk, u, A_WO + 2)
                    pool.tensor_tensor(L1.y[:, c % 2, :], g1[:], k.xt[:, at(c)], ALU.add).then_inc(L1.y_ready, 1)
            items(pool, step)


def stage_d_route(nc, k, a):
    with ExitStack() as ctx:
        sb = lambda n, s, t=F32: ctx.enter_context(nc.sbuf_tensor("d_" + n, s, t))
        sem = cleared_later(nc, ctx, "d_")
        FAR = 8192.0
        ws = sb("ws", [P, E + 2 * FE])
        wsd = sb("wsd", [FE, D])
        row = sb("row", [P, 4, TPC, ROW])
        zt = sb("zt", [P, 2, CH])
        lg, sh, ex, em = (sb(n, [P, 2, TPC, E]) for n in ("lg", "sh", "ex", "em"))
        rest_, mask = sb("rest", [P, TPC, E]), sb("mask", [P, 2, TPC, E])
        maskb, macc = sb("maskb", [P, 2, TPC, E], BF16), sb("macc", [P, 2, E], BF16)
        msum = sb("msum", [P, E])
        m8, den, rden = sb("m8", [P, TPC, 8]), sb("den", [P, TPC]), sb("rden", [P, TPC])
        far, place = sb("far", [P, TPC, E]), sb("place", [P, 2, TPC, E], BF16)
        hot = sb("hot", [P, 2, PAIRS * P], BF16)
        sg, hs = sb("sg", [FE, CH]), sb("hs", [FE, 2, CH])
        scan, scan_done = sb("scan", [P, TPC * E]), sem("scan_done")
        onesf = sb("onesf", [P, TPC * E])
        pay = sb("pay", [P, NT, 4], BF16)
        ps = k.ps
        L = Norm(nc, ctx, sem, "d_ln", ps[5], ps[6], k.eps5, xn=row[:, :, :, 0:D], ring=4)
        w_in = sem("w_in")
        rows_out = [sem(f"rows_out{i}") for i in range(4)]
        (init, zt_done, lg_done, lgc_done, gate_done, up_done, silu_done, hs_done, down_done, base_done, top_done,
         sh_done, rep_done, ex_done, mask_done, em_done, den_done, rden_done, row_done, maskb_done, macc_done,
         msum_done, pos_done, far_done, place_done, hot_done, tab_done, pay_done) = map(
            sem, "init zt_done lg_done lgc_done gate_done up_done silu_done hs_done down_done base_done top_done "
                 "sh_done rep_done ex_done mask_done em_done den_done rden_done row_done maskb_done macc_done "
                 "msum_done pos_done far_done place_done hot_done tab_done pay_done".split())
        block = ctx.enter_context(nc.Block())
        at = lambda c: slice(c * CH, (c + 1) * CH)
        STEPS = NC + 6

        @block.sync
        def _(sp):
            sp.dma_start(ws[:], a["ws"]).then_inc(w_in, 16)
            sp.dma_start(wsd[:], a["wsd"]).then_inc(w_in, 16)
            for c in range(NC):
                sp.wait_ge(row_done, 2 * c + 2)
                sp.dma_start(k.rows[c * CH:(c + 1) * CH, :].rearrange("(j p) w -> p j w", p=P), row[:, c % 4, :, :])\
                    .then_inc(rows_out[c % 4], 16)
            for i in range(4):
                sp.wait_ge(rows_out[i], 16 * (NC // 4))

        @block.tensor
        def _(pe):
            pe.wait_ge(w_in, 32)
            for s in range(STEPS):
                c = s
                if c < NC:
                    norm_fwd(pe, k, L, c, c)
                c = s - 2
                if 0 <= c < NC:
                    pe.wait_ge(zt_done, c + 1)
                    if c >= 1:
                        pe.wait_ge(lgc_done, c)
                    for j in range(TPC):
                        mm = pe.matmul(ps[0][:, j * E:(j + 1) * E], zt[:, c % 2, j * P:(j + 1) * P], ws[:, 0:E], start=True, stop=True)
                    mm.then_inc(lg_done, 1)
                    if c >= 1:
                        pe.wait_ge(hs_done, c)
                    pe.matmul(ps[1][0:FE, :], ws[:, E:E + FE], zt[:, c % 2, :], start=True, stop=True).then_inc(gate_done, 1)
                    pe.matmul(ps[2][0:FE, :], ws[:, E + FE:E + 2 * FE], zt[:, c % 2, :], start=True, stop=True).then_inc(up_done, 1)
                c = s - 1
                if 0 <= c < NC:
                    wait_older(pe, zt_done, c, 1)
                    norm_back(pe, k, L, c, c)
                c = s - 3
                if 0 <= c < NC:
                    pe.wait_ge(hs_done, c + 1)
                    if c >= 1:
                        pe.wait_ge(base_done, c)
                    for j in range(TPC):
                        mm = pe.matmul(ps[3][:, j * D:(j + 1) * D], hs[:, c % 2, j * P:(j + 1) * P], wsd[:], start=True, stop=True)
                    mm.then_inc(down_done, 1)
                c = s - 4
                if 0 <= c < NC:
                    pe.wait_ge(maskb_done, c + 1)
                    if c >= 1:
                        pe.wait_ge(macc_done, c)
                        pe.wait_ge(far_done, c)
                    for j in range(TPC):
                        terms = [(k.tri, maskb[:, c % 2, j, :])] + [(k.ones, maskb[:, c % 2, i, :]) for i in range(j)]
                        if c >= 1:
                            terms.append((k.ones, macc[:, c % 2, :]))
                        for i, (m, v) in enumerate(terms):
                            mm = pe.matmul(ps[4][:, j * E:(j + 1) * E], m[:], v, start=i == 0, stop=i == len(terms) - 1)
                    mm.then_inc(pos_done, 1)
                c = s - 5
                if 0 <= c < NC:
                    pe.wait_ge(pay_done, 1)
                    for j in range(TPC):
                        t = c * TPC + j
                        pe.wait_ge(hot_done, t + 1)
                        for g in range(PAIRS):
                            mm = pe.matmul(ps[7][:, 4 * g:4 * g + 4], hot[:, t % 2, g * P:(g + 1) * P], pay[:, t, :],
                                           start=(t == 0 and g == 0), stop=(t == NT - 1), skip_group_check=True)
                        mm.then_inc(tab_done, 1)

        @block.scalar
        def _(act):
            for s in range(STEPS):
                c = s - 2
                if 0 <= c < NC:
                    act.wait_ge(lg_done, c + 1)
                    if c >= 2:
                        act.wait_ge(mask_done, c - 1)
                    act.activation(lg[:, c % 2, :, :], ps[0][:, 0:TPC * E].rearrange("p (j e) -> p j e", e=E), ACT.Copy).then_inc(lgc_done, 1)
                    act.wait_ge(gate_done, c + 1)
                    if c >= 1:
                        act.wait_ge(hs_done, c)
                    act.activation(sg[:], ps[1][0:FE, :], ACT.Silu).then_inc(silu_done, 1)
                c = s - 1
                if 0 <= c < NC:
                    act.wait_ge(L.back_done, c + 1)
                    if c >= 2:
                        act.wait_ge(up_done, c - 1)
                    act.activation(zt[:, c % 2, :], L.back[:], ACT.Copy).then_inc(zt_done, 1)
                c = s - 3
                if 0 <= c < NC:
                    act.wait_ge(sh_done, c + 1)
                    if c >= 2:
                        act.wait_ge(em_done, c - 1)
                    act.activation(ex[:, c % 2, :, :], sh[:, c % 2, :, :], ACT.Exp).then_inc(ex_done, 1)

        @block.vector
        def _(dve):
            dve.memset(onesf[:], 1.0).then_inc(init, 1)
            dve.wait_ge(init, 1)
            for s in range(STEPS):
                c = s - 1
                if 0 <= c < NC:
                    if c >= 4:
                        dve.wait_ge(rows_out[c % 4], 16 * (c // 4))
                        dve.wait_ge(base_done, c - 3)
                    norm_apply(dve, k, L, c, c)
                c = s - 5
                if 0 <= c < NC:
                    dve.wait_ge(place_done, c + 1)
                    for j in range(TPC):
                        t = c * TPC + j
                        if t >= 2:
                            dve.wait_ge(tab_done, t - 1)
                        full = [P, PAIRS, CAP, 2]
                        dve.tensor_tensor(hot[:, t % 2, :].rearrange("p (g c q) -> p g c q", g=PAIRS, q=2),
                                          k.place_of[:].rearrange("p (c q) -> p c q", q=2).unsqueeze(1).to_broadcast(full),
                                          place[:, c % 2, j, :].rearrange("p (g q) -> p g q", q=2).unsqueeze(2).to_broadcast(full),
                                          ALU.is_equal).then_inc(hot_done, 1)
                c = s - 4
                if 0 <= c < NC:
                    dve.wait_ge(pos_done, c + 1)
                    dve.scalar_tensor_tensor(far[:], mask[:, c % 2, :, :], -FAR, ps[4][:, 0:TPC * E].rearrange("p (j e) -> p j e", e=E),
                                             ALU.mult, ALU.add).then_inc(far_done, 1)
                    dve.wait_ge(far_done, c + 1)
                    dve.tensor_scalar(place[:, c % 2, :, :], far[:], FAR, None, ALU.add).then_inc(place_done, 1)
                c = s
                if c < NC:
                    norm_stats(dve, k, L, c, c)
                c = s - 2
                if 0 <= c < NC:
                    dve.wait_ge(silu_done, c + 1)
                    dve.wait_ge(up_done, c + 1)
                    if c >= 2:
                        dve.wait_ge(down_done, c - 1)
                    dve.tensor_tensor(hs[:, c % 2, :], sg[:], ps[2][0:FE, :], ALU.mult).then_inc(hs_done, 1)
                c = s - 3
                if 0 <= c < NC:
                    l = lg[:, c % 2, :, :]
                    dve.wait_ge(lgc_done, c + 1)
                    for j in range(TPC):
                        i = dve.max(m8[:, j, :], l[:, j, :])
                    i.then_inc(top_done, 1)
                    dve.wait_ge(top_done, c + 1)
                    dve.tensor_tensor(sh[:, c % 2, :, :], l, m8[:, :, 0:1].to_broadcast([P, TPC, E]), ALU.subtract).then_inc(sh_done, 1)
                    for j in range(TPC):
                        i = dve.match_replace(rest_[:, j, :], m8[:, j, :], l[:, j, :], -3e38)
                    i.then_inc(rep_done, 1)
                    dve.wait_ge(rep_done, c + 1)
                    if c >= 2:
                        dve.wait_ge(far_done, c - 1)
                    dve.tensor_tensor(mask[:, c % 2, :, :], rest_[:], l, ALU.not_equal).then_inc(mask_done, 1)
                    dve.wait_ge(mask_done, c + 1)
                    if c >= 2:
                        dve.wait_ge(pos_done, c - 1)
                    dve.tensor_copy(maskb[:, c % 2, :, :], mask[:, c % 2, :, :]).then_inc(maskb_done, 1)
                    dve.tensor_tensor_scan(scan[:], onesf[:], mask[:, c % 2, :, :].rearrange("p j e -> p (j e)"), 0.0, ALU.mult, ALU.add).then_inc(scan_done, 1)
                    dve.wait_ge(ex_done, c + 1)
                    dve.tensor_tensor(em[:, c % 2, :, :], ex[:, c % 2, :, :], mask[:, c % 2, :, :], ALU.mult).then_inc(em_done, 1)
                    dve.wait_ge(em_done, c + 1)
                    dve.tensor_reduce(den[:], em[:, c % 2, :, :], AX.X, ALU.add).then_inc(den_done, 1)
                    dve.tensor_reduce(msum[:], mask[:, c % 2, :, :].rearrange("p j e -> p e j"), AX.X, ALU.add).then_inc(msum_done, 1)
                    dve.wait_ge(den_done, c + 1)
                    dve.reciprocal(rden[:], den[:]).then_inc(rden_done, 1)
                    dve.wait_ge(scan_done, c + 1)
                    dve.tensor_copy(row[:, c % 4, :, D + E:ROW], scan[:].rearrange("p (j e) -> p j e", e=E)).then_inc(row_done, 1)
                    dve.wait_ge(rden_done, c + 1)
                    dve.tensor_tensor(row[:, c % 4, :, D:D + E], em[:, c % 2, :, :],
                                      rden[:].unsqueeze(2).to_broadcast([P, TPC, E]), ALU.mult).then_inc(row_done, 1)
                    dve.wait_ge(msum_done, c + 1)
                    if c >= 1:
                        dve.wait_ge(macc_done, c)
                        dve.wait_ge(pos_done, c)
                        dve.tensor_tensor(macc[:, (c + 1) % 2, :], msum[:], macc[:, c % 2, :], ALU.add).then_inc(macc_done, 1)
                    else:
                        dve.tensor_copy(macc[:, 1, :], msum[:]).then_inc(macc_done, 1)
                    dve.wait_ge(down_done, c + 1)
                    dve.tensor_tensor(k.base[:, c * TPC:(c + 1) * TPC, :], ps[3][:].rearrange("p (j d) -> p j d", d=D),
                                      row[:, c % 4, :, 0:D], ALU.add).then_inc(base_done, 1)

        @block.gpsimd
        def _(pool):
            for t in range(NT):
                pool.memset(pay[:, t, 0:1], float(t))
                pool.memset(pay[:, t, 3:4], float(t % TPC))
            pool.memset(pay[:, :, 2:3], 1.0)
            pool.tensor_copy(pay[:, :, 1], k.iota_pf[:].to_broadcast([P, NT])).then_inc(pay_done, 1)
            for s in range(STEPS):
                c = s
                if c < NC:
                    if c >= 2:
                        pool.wait_ge(L.fwd_done, c - 1)
                    pool.tensor_tensor(L.y[:, c % 2, :], k.xt0[:, at(c)], k.xt[:, at(c)], ALU.add).then_inc(L.y_ready, 1)
                    norm_rstd(pool, k, L, c, c)


def stage_d_experts(nc, k, a):
    U = 4
    with ExitStack() as ctx:
        sb = lambda n, s, t=F32: ctx.enter_context(nc.sbuf_tensor("e_" + n, s, t))
        sem = cleared_later(nc, ctx, "e_")
        sems = lambda n: [sem(f"{n}{i}") for i in range(U)]
        tab = sb("tab", [P, PAIRS, 4])
        tok, tok8, none, dest0 = (sb(n, [P, PAIRS]) for n in ("tok", "tok8", "none", "dest0"))
        token = sb("token", [P, PAIRS], I32)
        idx, dest = sb("idx", [P, U, 1], I32), sb("dest", [P, U, 1], I32)
        got = sb("got", [P, U, ROW])
        picks, pick = sb("picks", [P, U, 2, 2]), sb("pick", [P, U, 2])
        wgu, wd = sb("wgu", [P, U, 2, 2 * FE]), sb("wd", [FE, U, 2, D])
        xb = sb("xb", [P, 2, P])
        sg, h = sb("sg", [FE, 2, P]), sb("h", [FE, 2, 2, P])
        y = sb("y", [P, U, D])
        FARROW = 65536.0
        ps = k.ps
        w_in, g_in, s_out = sems("w_in"), sems("g_in"), sems("s_out")
        (prep, idx_done, tr_done, xb_done, picks_done, pick_done, dest_done, gu_done, silu_done, h_done, yp_done, y_done) = map(
            sem, "prep idx_done tr_done xb_done picks_done pick_done dest_done gu_done silu_done h_done yp_done y_done".split())
        block = ctx.enter_context(nc.Block())
        DEPTH = 5
        L_GOT, L_GU, L_Y, L_SC = 2, 3, 4, 5

        @block.sync
        def _(sp):
            def step(kk, u):
                if live(kk, u, 0, PAIRS, U):
                    g, t, r = lagged(kk, u, 0, U)
                    if beyond(t, U):
                        sp.wait_ge(yp_done, t - U + 1)
                    sp.dma_start(wgu[:, r, :, :], a["wgu"][bass.ds(t * P, P), :].rearrange("p (h w) -> p h w", h=2)).then_inc(w_in[r], 16)
                    sp.dma_start(wd[:, r, :, :], a["wd"][bass.ds(t * FE, FE), :].rearrange("p (h w) -> p h w", h=2)).then_inc(w_in[r], 16)
            steps(sp, PAIRS, DEPTH, step, U)

        @block.gpsimd
        def _(pool):
            def step(kk, u):
                if live(kk, u, 0, PAIRS, U):
                    g, t, r = lagged(kk, u, 0, U)
                    pool.wait_ge(idx_done, t + 1)
                    if beyond(t, U):
                        pool.wait_ge(tr_done, t - U + 1)
                        pool.wait_ge(picks_done, t - U + 1)
                    pool.indirect_dma_start(got[:, r, :], None, k.rows, bass.IndirectOffsetOnAxis(ap=idx[:, r, :], axis=0)).then_inc(g_in[r], 16)
                if live(kk, u, L_SC, PAIRS, U):
                    g, t, r = lagged(kk, u, L_SC, U)
                    pool.wait_ge(dest_done, t + 1)
                    pool.wait_ge(y_done, t + 1)
                    pool.indirect_dma_start(k.contrib, bass.IndirectOffsetOnAxis(ap=dest[:, r, :], axis=0), y[:, r, :], None,
                                            bounds_check=DUMP - 1, oob_is_err=False).then_inc(s_out[r], 16)
            steps(pool, PAIRS, DEPTH, step, U, rolled=False)
            for i in range(U):
                pool.wait_ge(s_out[i], 16 * (PAIRS // U))

        @block.tensor
        def _(pe):
            def step(kk, u):
                if live(kk, u, L_GOT, PAIRS, U):
                    g, t, r = lagged(kk, u, L_GOT, U)
                    pe.wait_ge(g_in[r], g * 16 + 16)
                    if beyond(t, 1):
                        pe.wait_ge(xb_done, t)
                    pe.transpose(ps[0][:, 0:P], got[:, r, 0:D], k.ident[:]).then_inc(tr_done, 1)
                if live(kk, u, L_Y, PAIRS, U):
                    g, t, r = lagged(kk, u, L_Y, U)
                    pe.wait_ge(h_done, t + 1)
                    if beyond(t, 2):
                        pe.wait_ge(y_done, t - 1)
                    for e in range(2):
                        mm = pe.matmul(ps[3 + r % 2][:, 0:D], h[:, r % 2, e, :], wd[:, r, e, :], start=e == 0, stop=e == 1)
                    mm.then_inc(yp_done, 1)
                if live(kk, u, L_GU, PAIRS, U):
                    g, t, r = lagged(kk, u, L_GU, U)
                    pe.wait_ge(xb_done, t + 1)
                    pe.wait_ge(w_in[r], g * 32 + 32)
                    if beyond(t, 2):
                        pe.wait_ge(h_done, t - 1)
                    for q in range(2):
                        for e in range(2):
                            mm = pe.matmul(ps[1 + r % 2][0:FE, (2 * q + e) * CAP:(2 * q + e + 1) * CAP], wgu[:, r, e, q * FE:(q + 1) * FE],
                                           xb[:, r % 2, e:P:2], start=True, stop=True)
                    mm.then_inc(gu_done, 1)
            steps(pe, PAIRS, DEPTH, step, U)

        @block.scalar
        def _(act):
            def step(kk, u):
                if live(kk, u, L_Y, PAIRS, U):
                    g, t, r = lagged(kk, u, L_Y, U)
                    act.wait_ge(yp_done, t + 1)
                    act.wait_ge(pick_done, t + 1)
                    if beyond(t, U):
                        act.wait_ge(s_out[r], g * 16)
                    act.activation(y[:, r, :], ps[3 + r % 2][:, 0:D], ACT.Copy, scale=pick[:, r, 0:1]).then_inc(y_done, 1)
                if live(kk, u, L_GU, PAIRS, U):
                    g, t, r = lagged(kk, u, L_GU, U)
                    act.wait_ge(gu_done, t + 1)
                    if beyond(t, 2):
                        act.wait_ge(h_done, t - 1)
                    act.activation(sg[:, r % 2, :], ps[1 + r % 2][0:FE, 0:P], ACT.Silu).then_inc(silu_done, 1)
                if live(kk, u, L_GOT, PAIRS, U):
                    g, t, r = lagged(kk, u, L_GOT, U)
                    act.wait_ge(tr_done, t + 1)
                    if beyond(t, 2):
                        act.wait_ge(gu_done, t - 1)
                    act.activation(xb[:, r % 2, :], ps[0][:, 0:P], ACT.Copy).then_inc(xb_done, 1)
            steps(act, PAIRS, DEPTH, step, U)

        @block.vector
        def _(dve):
            n = [0]

            def chain(i):
                i.then_inc(prep, 1)
                n[0] += 1
                dve.wait_ge(prep, n[0])
            chain(dve.memset(h[:], 0.0))
            chain(dve.tensor_copy(tab[:].rearrange("p g w -> p (g w)"), ps[7][:, 0:4 * PAIRS]))
            chain(dve.scalar_tensor_tensor(tok[:], tab[:, :, 0], float(TILE), tab[:, :, 1], ALU.mult, ALU.add))
            chain(dve.tensor_copy(token[:], tok[:]))
            chain(dve.tensor_scalar(tok8[:], tok[:], float(TOPK), -1.0, ALU.mult, ALU.add))
            chain(dve.tensor_scalar(none[:], tab[:, :, 2], -FARROW, FARROW, ALU.mult, ALU.add))
            chain(dve.tensor_tensor(tok8[:], tok8[:], none[:], ALU.add))
            chain(dve.scalar_tensor_tensor(dest0[:], tab[:, :, 3], -float(TOPK), tok8[:], ALU.mult, ALU.add))

            def step(kk, u):
                if live(kk, u, 0, PAIRS, U):
                    g, t, r = lagged(kk, u, 0, U)
                    if beyond(t, U):
                        dve.wait_ge(g_in[r], g * 16)
                    dve.tensor_copy(idx[:, r, :], token[:, bass.ds(t, 1)]).then_inc(idx_done, 1)
                if live(kk, u, L_GOT, PAIRS, U):
                    g, t, r = lagged(kk, u, L_GOT, U)
                    dve.wait_ge(g_in[r], g * 16 + 16)
                    if beyond(t, U):
                        dve.wait_ge(pick_done, t - U + 1)
                    wr = got[:, r, D:ROW].rearrange("p (q e) -> p q e", q=2)[:, :, bass.ds(t * 2, 2)]
                    dve.tensor_tensor(picks[:, r, :, :], wr, k.parmask[:].unsqueeze(1).to_broadcast([P, 2, 2]), ALU.mult).then_inc(picks_done, 1)
                    if beyond(t, U):
                        dve.wait_ge(y_done, t - U + 1)
                    dve.wait_ge(picks_done, t + 1)
                    dve.tensor_reduce(pick[:, r, :], picks[:, r, :, :], AX.X, ALU.add).then_inc(pick_done, 1)
                    if beyond(t, U):
                        dve.wait_ge(s_out[r], g * 16)
                    dve.wait_ge(pick_done, t + 1)
                    dve.tensor_tensor(dest[:, r, :], pick[:, r, 1:2], dest0[:, bass.ds(t, 1)], ALU.add).then_inc(dest_done, 1)
                if live(kk, u, L_GU, PAIRS, U):
                    g, t, r = lagged(kk, u, L_GU, U)
                    dve.wait_ge(silu_done, t + 1)
                    if beyond(t, 2):
                        dve.wait_ge(yp_done, t - 1)
                    for e in range(2):
                        cols = slice(e * CAP, (e + 1) * CAP)
                        i = dve.tensor_tensor(h[:, r % 2, e, e:P:2], sg[:, r % 2, cols], ps[1 + r % 2][0:FE, P + e * CAP:P + (e + 1) * CAP], ALU.mult)
                    i.then_inc(h_done, 1)
            steps(dve, PAIRS, DEPTH, step, U)


def stage_d_sum(nc, k, a):
    U = 4
    with ExitStack() as ctx:
        sb = lambda n, s, t=F32: ctx.enter_context(nc.sbuf_tensor("f_" + n, s, t))
        sem = cleared_later(nc, ctx, "f_")
        sems = lambda n: [sem(f"{n}{i}") for i in range(U)]
        st, mv, var, rstd, mark = sb("st", [P, 2, 6]), sb("mv", [P, 4, 2]), sb("var", [P, 2, 1]), sb("rstd", [P, 4, 1]), sb("mark", [P, 1])
        con = sb("con", [P, U, TOPK, D])
        tot, y, out = sb("tot", [P, 2, D]), sb("y", [P, 4, D]), sb("out", [P, U, D])
        c_in, o_out = sems("c_in"), sems("o_out")
        clean = sem("clean")
        (tot_done, y_done, st_done, mv_done, var_done, rstd_done, out_done) = map(
            sem, "tot_done y_done st_done mv_done var_done rstd_done out_done".split())
        block = ctx.enter_context(nc.Block())
        DEPTH = 4
        L_SUM, L_OUT = 2, 3
        contrib = k.contrib.rearrange("(t r) d -> t (r d)", r=TOPK)

        @block.sync
        def _(sp):
            def step(kk, u):
                if live(kk, u, 0, NT, U):
                    g, t, r = lagged(kk, u, 0, U)
                    if beyond(t, U):
                        sp.wait_ge(tot_done, t - U + 1)
                    sp.dma_start(con[:, r, :, :].rearrange("p r d -> p (r d)"), contrib[bass.ds(t * P, P), :]).then_inc(c_in[r], 16)
            steps(sp, NT, DEPTH, step, U)

        @block.scalar
        def _(act):
            def step(kk, u):
                if live(kk, u, L_OUT, NT, U):
                    g, t, r = lagged(kk, u, L_OUT, U)
                    act.wait_ge(out_done, t + 1)
                    act.dma_start(a["out"][bass.ds(t * P, P), :], out[:, r, :]).then_inc(o_out[r], 16)
            steps(act, NT, DEPTH, step, U)
            for i in range(U):
                act.wait_ge(o_out[i], 16 * (NT // U))

        @block.vector
        def _(dve):
            dve.memset(mv[:], 0.0).then_inc(clean, 1)
            dve.wait_ge(clean, 1)

            def step(kk, u):
                if live(kk, u, L_OUT, NT, U):
                    g, t, r = lagged(kk, u, L_OUT, U)
                    dve.wait_ge(rstd_done, t + 1)
                    if beyond(t, U):
                        dve.wait_ge(o_out[r], g * 16)
                    dve.tensor_scalar(out[:, r, :], y[:, r, :], mv[:, r, 0:1], rstd[:, r, :], ALU.subtract, ALU.mult).then_inc(out_done, 1)
                if live(kk, u, L_SUM, NT, U):
                    g, t, r = lagged(kk, u, L_SUM, U)
                    dve.wait_ge(c_in[r], g * 16 + 16)
                    if beyond(t, 2):
                        dve.wait_ge(y_done, t - 1)
                    dve.tensor_reduce(tot[:, r % 2, :], con[:, r, :, :].rearrange("p r d -> p d r"), AX.X, ALU.add).then_inc(tot_done, 1)
                    dve.wait_ge(tot_done, t + 1)
                    if beyond(t, U):
                        dve.wait_ge(out_done, t - U + 1)
                    dve.tensor_tensor(y[:, r, :], tot[:, r % 2, :], k.base[:, bass.ds(t, 1), :].rearrange("p o d -> p (o d)"), ALU.add).then_inc(y_done, 1)
                    dve.wait_ge(y_done, t + 1)
                    if beyond(t, 2):
                        dve.wait_ge(mv_done, t - 1)
                    dve.bn_stats(st[:, r % 2, :], y[:, r, :]).then_inc(st_done, 1)
                    dve.wait_ge(st_done, t + 1)
                    dve.tensor_copy(mark[:], st[:, r % 2, 0:1])
                    dve.bn_aggr(mv[:, r, :], st[:, r % 2, :]).then_inc(mv_done, 1)
            steps(dve, NT, DEPTH, step, U)

        @block.gpsimd
        def _(pool):
            def step(kk, u):
                if live(kk, u, L_SUM, NT, U):
                    g, t, r = lagged(kk, u, L_SUM, U)
                    pool.wait_ge(mv_done, t + 1)
                    if beyond(t, 2):
                        pool.wait_ge(rstd_done, t - 1)
                    pool.tensor_tensor(var[:, r % 2, :], mv[:, r, 1:2], k.eps5[:, 0:1], ALU.add).then_inc(var_done, 1)
                    if beyond(t, U):
                        pool.wait_ge(out_done, t - U + 1)
                    pool.wait_ge(var_done, t + 1)
                    pool.tensor_tensor(rstd[:, r, :], var[:, r % 2, :], k.mhalf[:, 0:1], ALU.pow).then_inc(rstd_done, 1)
            steps(pool, NT, DEPTH, step, U)


def build(nc, a):
    with ExitStack() as ctx:
        k = Shared(nc, ctx)
        constants(nc, k, a)
        stage_a(nc, k, a)
        stage_b(nc, k, a)
        stage_c(nc, k, a)
        stage_d_route(nc, k, a)
        stage_d_experts(nc, k, a)
        stage_d_sum(nc, k, a)


def layout(x):
    import numpy as np
    c = np.ascontiguousarray
    t = lambda w: np.swapaxes(w, -1, -2)
    x = {n: np.asarray(v) for n, v in x.items()}
    tok = x["L0_attn_x"].reshape(TOKENS, D)
    out = {
        "x": c(tok), "xt": c(tok.T),
        "wqkv": c(np.concatenate([x["L0_attn_Wq"].T, x["L0_attn_Wk"].T, x["L0_attn_Wv"].T], 1)),
        "wfc": c(x["L0_attn_Wfc"].T),
    }
    out["wffn"] = c(np.concatenate([x["L0_ffn_w_gate"].T, x["L0_ffn_w_up"].T]
                    + [x["L0_ffn_w_down"][:, j * P:(j + 1) * P].T for j in range(NJ)], 1))
    v = {n[8:]: w for n, w in x.items() if n.startswith("L1_attn_")}
    col = lambda n: v[n][:, :, None]
    out["w1"] = c(np.concatenate([v["Wq"], v["Wk"], v["Wv"], col("bq"), col("bk"), col("bv")], 2).reshape(BLOCKS * P, W1COLS))
    w2r = v["W2"].reshape(BLOCKS, NF, P, D).transpose(0, 2, 1, 3).reshape(BLOCKS, P, NF * D)
    b1r = v["b1"].reshape(BLOCKS, NF, P).transpose(0, 2, 1)
    out["w2"] = c(np.concatenate([v["Wo"], col("bo"), v["W1"], b1r, col("ln1_s"), col("ln1_b"), w2r, col("b2"),
                                  col("ln2_s"), col("ln2_b")], 2).reshape(BLOCKS * P, W2COLS))
    f = {n[7:]: w for n, w in x.items() if n.startswith("L1_ffn_")}
    out["ws"] = c(np.concatenate([f["router_w"].T, f["ws_gate_up"]], 1))
    out["wsd"] = c(f["ws_down"])
    pair = lambda w, m: w.reshape(PAIRS, 2, m, -1).transpose(0, 2, 1, 3).reshape(PAIRS * m, -1)
    out["wgu"] = c(pair(np.concatenate([f["w_gate"], f["w_up"]], 2), D))
    out["wd"] = c(pair(f["w_down"], FE))
    return out


def kernel(**inputs):
    import concourse.bacc as bacc
    import numpy as np
    from concourse.bass_utils import run_bass_kernel_spmd

    nc = bacc.Bacc("TRN2", target_bir_lowering=False, num_devices=1)
    arrays = layout(inputs)
    a = {n: nc.dram_tensor("in_" + n, v.shape, mybir.dt.from_np(v.dtype), kind="ExternalInput").ap() for n, v in arrays.items()}
    a["out"] = nc.dram_tensor("out_0", [TOKENS, D], F32, kind="ExternalOutput").ap()
    build(nc, a)
    r = run_bass_kernel_spmd(nc, [{"in_" + n: v for n, v in arrays.items()}], core_ids=[0])
    return np.asarray(r.results[0]["out_0"]).reshape(8, CH, D)
```

```python
from contextlib import ExitStack

import concourse.bass as bass
from concourse import mybir

F32 = mybir.dt.float32
BF16 = mybir.dt.bfloat16
I32 = mybir.dt.int32
U32 = mybir.dt.uint32
ALU = mybir.AluOpType
ACT = mybir.ActivationFunctionType
AX = mybir.AxisListType

P = 128
D = 128
TOKENS = 8 * 512
TILE = 128
NT = TOKENS // TILE
CH = 512
NC = TOKENS // CH
TPC = CH // TILE
HEADS, HD = 16, 8
HIDDEN, NJ = 384, 3
BLOCKS = 8
FF, NF = 512, 4
E, TOPK, CAP, FE = 64, 8, 64, 96
PAIRS = E // 2
ROW = D + 2 * E
DUMP = TOKENS * TOPK
EXP_LN_SET = "natural_log_exp_and_others"
GELU_SET = "gelu_apprx_tanh_and_others"
W1COLS = 3 * D + 3
O_LN1 = D + 1
O_F1 = O_LN1 + 2
O_F2 = O_F1 + FF + NF
O_LN2 = O_F2 + NF * D + 1
W2COLS = O_LN2 + 2


def lagged(k, u, lag, unroll=2):
    r = (u - lag) % unroll
    g = k + (u - lag - r) // unroll
    return g, g * unroll + r, r


def live(k, u, lag, n, unroll=2):
    return not isinstance(k, int) or 0 <= k * unroll + u - lag < n


def steps(eng, n, depth, body, unroll=2, ring=None, rolled=True):
    head = min(-(-(depth + (ring or unroll)) // unroll), n // unroll) if rolled else n // unroll
    for k in range(head):
        for u in range(unroll):
            body(k, u)
    if head < n // unroll:
        with eng.Fori(head, n // unroll) as k:
            for u in range(unroll):
                body(k, u)
    for s in range(n, n + depth):
        body(s // unroll, s % unroll)


def beyond(t, n):
    return not isinstance(t, int) or t >= n


class Shared:

    def __init__(self, nc, ctx):
        sb = lambda n, s, t=F32: ctx.enter_context(nc.sbuf_tensor(n, s, t))
        self.ps = [ctx.enter_context(nc.psum_tensor(f"bank{i}", [P, 512], F32)) for i in range(8)]
        self.ident = sb("ident", [P, P])
        self.tri, self.ones = sb("tri", [P, P], BF16), sb("ones", [P, P], BF16)
        self.parmask = sb("parmask", [P, 2])
        self.eps5, self.eps6, self.mhalf = sb("eps5", [P, TPC]), sb("eps6", [P, TPC]), sb("mhalf", [P, TPC])
        self.iota_p, self.iota_pf = sb("iota_p", [P, 1], I32), sb("iota_pf", [P, 1])
        self.iota_c, self.place_of = sb("iota_c", [P, CAP], I32), sb("place_of", [P, P], BF16)
        self.xt, self.xt0 = sb("xt", [P, TOKENS]), sb("xt0", [P, TOKENS])
        self.base = sb("base", [P, NT, D])
        self.zeros = sb("zeros", [P, 2048])
        self.wqkv_a, self.wfc = sb("wqkv_a", [P, 3 * D]), sb("wfc", [P, D])
        self.wffn = sb("wffn", [P, 3 * HIDDEN], I32)
        self.wqkv, self.wo = sb("wqkv", [P, W1COLS]), sb("wo", [P, D + 1])
        self.wf1, self.wf2 = sb("wf1", [P, FF + NF]), sb("wf2", [P, NF * D + 1])
        self.ln1, self.ln2 = sb("ln1", [P, 2]), sb("ln2", [P, 2])
        self.ws, self.wsd = sb("ws", [P, E + 2 * FE]), sb("wsd", [FE, D])
        self.wa_in, self.wffn_in, self.ws_in, self.wqkv_in, self.wo_in, self.wf1_in, self.wf2_in, self.ln1_in, self.ln2_in = (
            ctx.enter_context(nc.semaphore(n)) for n in (
                "wa_in", "wffn_in", "ws_in", "wqkv_in", "wo_in", "wf1_in", "wf2_in", "ln1_in", "ln2_in"))
        self.rows = nc.dram_tensor("rows", [TOKENS, ROW], F32).ap()
        self.contrib = nc.dram_tensor("contrib", [DUMP, D], F32).ap()
        self.x_ready = ctx.enter_context(nc.semaphore("x_ready"))


def constants(nc, k, a):
    with ExitStack() as ctx:
        s_zero = ctx.enter_context(nc.semaphore("c_zero"))
        s_sel = ctx.enter_context(nc.semaphore("c_sel"))
        s_iota = ctx.enter_context(nc.semaphore("c_iota"))
        s_eps = ctx.enter_context(nc.semaphore("c_eps"))
        block = ctx.enter_context(nc.Block())

        @block.sync
        def _(sp):
            sp.dma_start(k.wqkv_a[:], a["wqkv"]).then_inc(k.wa_in, 16)
            sp.dma_start(k.wfc[:], a["wfc"]).then_inc(k.wa_in, 16)

        @block.gpsimd
        def _(pool):
            pool.memset(k.ident[:], 0.0).then_inc(s_zero, 1)
            pool.memset(k.tri[:], 1.0).then_inc(s_zero, 1)
            pool.memset(k.ones[:], 1.0).then_inc(s_zero, 1)
            pool.wait_ge(s_zero, 3)
            pool.affine_select(out=k.ident[:], in_=k.ident[:], compare_op=ALU.not_equal, fill=1.0,
                               base=0, pattern=[[-1, P]], channel_multiplier=1).then_inc(s_sel, 1)
            pool.affine_select(out=k.tri[:], in_=k.tri[:], compare_op=ALU.is_gt, fill=0.0,
                               base=0, pattern=[[1, P]], channel_multiplier=-1).then_inc(s_sel, 1)
            pool.iota(k.iota_p[:], pattern=[[0, 1]], base=0, channel_multiplier=1).then_inc(s_iota, 1)
            pool.iota(k.iota_c[:], pattern=[[1, CAP]], base=0, channel_multiplier=0).then_inc(s_iota, 1)

        @block.vector
        def _(dve):
            dve.memset(k.eps5[:], 1e-5).then_inc(s_eps, 1)
            dve.memset(k.zeros[:], 0.0).then_inc(s_eps, 1)
            dve.memset(k.eps6[:], 1e-6).then_inc(s_eps, 1)
            dve.memset(k.mhalf[:], -0.5).then_inc(s_eps, 1)
            dve.wait_ge(s_iota, 2)
            dve.tensor_copy(k.place_of[:].rearrange("p (c q) -> p c q", q=2),
                            k.iota_c[:].unsqueeze(2).to_broadcast([P, CAP, 2])).then_inc(s_eps, 1)
            dve.wait_ge(s_sel, 2)
            dve.tensor_reduce(k.parmask[:], k.ident[:].rearrange("p (m q) -> p q m", q=2), AX.X, ALU.add).then_inc(s_eps, 1)
            dve.tensor_copy(k.iota_pf[:], k.iota_p[:]).then_inc(s_eps, 1)


def cleared_later(nc, ctx, prefix):
    made = []

    def clear():
        nc.clear_and_free_semaphores(made)
        nc.all_engine_barrier()
    ctx.callback(clear)

    def sem(name):
        made.append(nc.alloc_semaphore(name=prefix + name))
        return made[-1]
    return sem


def stage_a(nc, k, a):
    with ExitStack() as ctx:
        sb = lambda n, s, t=F32: ctx.enter_context(nc.sbuf_tensor("a_" + n, s, t))
        sem = cleared_later(nc, ctx, "a_")
        x_in = sb("x_in", [P, 4, TILE])
        x_res = sb("x_res", [P, 4, D])
        qkv = sb("qkv", [P, 4, 3 * D])
        prod = sb("prod", [P, 2, HD, HEADS * HEADS])
        top = sb("top", [P, 2, HEADS])
        shifted = sb("shifted", [P, 2, 256])
        expd = sb("expd", [P, 2, 256])
        den, rden = sb("den", [P, 4, HEADS]), sb("rden", [P, 4, HEADS])
        pv = sb("pv", [P, 2, HEADS, D])
        pvh = sb("pvh", [P, 2, HEADS // 2, D])
        o_nat, o_t = sb("o_nat", [P, 2, D]), sb("o_t", [P, 2, TILE])
        y, st, mv, rstd, xn = sb("y", [P, 2, D]), sb("st", [P, 2, 6]), sb("mv", [P, 2, 2]), sb("rstd", [P, 2, 1]), sb("xn", [P, 2, D])
        ps = k.ps
        x_here = [sem(f"x_here{i}") for i in range(4)]
        r_here = [sem(f"r_here{i}") for i in range(4)]
        (qkv_done, qkv_sb, prod_done, score_done, shift_done, exp_done, pvp_done, half_done, pv_done,
         norm_done, ot_done, ot_sb, fc_done, stat_done, rstd_done, xn_done, back_done, xt_done, dsem) = map(
            sem, "qkv_done qkv_sb prod_done score_done shift_done exp_done pvp_done half_done pv_done "
                 "norm_done ot_done ot_sb fc_done stat_done rstd_done xn_done back_done xt_done dsem".split())
        var, var_done = sb("var", [P, 2, 1]), sem("var_done")
        soft, topped, rden_done = sem("soft"), sem("topped"), sem("rden_done")
        block = ctx.enter_context(nc.Block())
        U, DEPTH = 4, 10
        L_QK, L_SC, L_PVP, L_PV, L_NORM, L_OT, L_FC, L_LN, L_XN, L_BACK = 1, 2, 3, 4, 5, 6, 7, 8, 9, 10
        NDVE = 6

        @block.sync
        def _(sp):

            def step(kk, u):
                if live(kk, u, 0, NT, U):
                    g, t, q = lagged(kk, u, 0, U)
                    r = q % 2
                    if beyond(t, 4):
                        sp.wait_ge(qkv_done, t - 3)
                    sp.dma_start(x_in[:, q, :], a["xt"][:, bass.ds(t * TILE, TILE)]).then_inc(x_here[q], 16)
                if live(kk, u, L_FC, NT, U):
                    g, t, q = lagged(kk, u, L_FC, U)
                    r = q % 2
                    if beyond(t, 4):
                        sp.wait_ge(dsem, (t - 4) * 2 + 1)
                    sp.dma_start(x_res[:, q, :], a["x"][bass.ds(t * TILE, TILE), :]).then_inc(r_here[q], 16)
            steps(sp, NT, DEPTH, step, U, ring=4)
            sp.dma_start(k.wffn[:], a["wffn"]).then_inc(k.wffn_in, 16)

        @block.tensor
        def _(pe):
            pe.wait_ge(k.wa_in, 32)

            def step(kk, u):
                if live(kk, u, L_SC, NT, U):
                    g, t, q = lagged(kk, u, L_SC, U)
                    r = q % 2
                    pe.wait_ge(prod_done, t + 1)
                    if beyond(t, 2):
                        pe.wait_ge(shift_done, t - 1)
                    for d in range(HD):
                        mm = pe.matmul(ps[2 + r][:, 0:256], k.ident[:], prod[:, r, d, :], start=d == 0, stop=d == HD - 1)
                    mm.then_inc(score_done, 1)
                if live(kk, u, 0, NT, U):
                    g, t, q = lagged(kk, u, 0, U)
                    r = q % 2
                    pe.wait_ge(x_here[q], g * 16 + 16)
                    if beyond(t, 2):
                        pe.wait_ge(qkv_sb, t - 1)
                    pe.matmul(ps[r][:, 0:3 * D], x_in[:, q, :], k.wqkv_a[:], start=True, stop=True).then_inc(qkv_done, 1)
                if live(kk, u, L_PV, NT, U):
                    g, t, q = lagged(kk, u, L_PV, U)
                    r = q % 2
                    pe.wait_ge(half_done, t + 1)
                    if beyond(t, 1):
                        pe.wait_ge(norm_done, t)
                    for j in range(HEADS // 2):
                        mm = pe.matmul(ps[4][:, 0:D], k.ident[:], pvh[:, r, j, :], start=j == 0, stop=j == HEADS // 2 - 1)
                    mm.then_inc(pv_done, 1)
                if live(kk, u, L_OT, NT, U):
                    g, t, q = lagged(kk, u, L_OT, U)
                    r = q % 2
                    pe.wait_ge(norm_done, t + 1)
                    if beyond(t, 1):
                        pe.wait_ge(ot_sb, t)
                    pe.transpose(ps[5][:, 0:TILE], o_nat[:, r, :], k.ident[:]).then_inc(ot_done, 1)
                if live(kk, u, L_FC, NT, U):
                    g, t, q = lagged(kk, u, L_FC, U)
                    r = q % 2
                    pe.wait_ge(ot_sb, t + 1)
                    if beyond(t, 1):
                        pe.wait_ge(dsem, t * 2 - 1)
                    pe.matmul(ps[6][:, 0:D], o_t[:, r, :], k.wfc[:], start=True, stop=True).then_inc(fc_done, 1)
                if live(kk, u, L_BACK, NT, U):
                    g, t, q = lagged(kk, u, L_BACK, U)
                    r = q % 2
                    pe.wait_ge(xn_done, t + 1)
                    if beyond(t, 1):
                        pe.wait_ge(xt_done, t)
                    pe.transpose(ps[7][:, 0:TILE], xn[:, r, :], k.ident[:]).then_inc(back_done, 1)
            steps(pe, NT, DEPTH, step, U, ring=4)

        @block.scalar
        def _(act):
            def step(kk, u):
                if live(kk, u, 0, NT, U):
                    g, t, q = lagged(kk, u, 0, U)
                    r = q % 2
                    act.wait_ge(qkv_done, t + 1)
                    if beyond(t, 4):
                        act.wait_ge(pvp_done, t - 3)
                    act.activation(qkv[:, q, :], ps[r][:, 0:3 * D], ACT.Copy).then_inc(qkv_sb, 1)
                if live(kk, u, L_SC, NT, U):
                    g, t, q = lagged(kk, u, L_SC, U)
                    r = q % 2
                    act.wait_ge(shift_done, t + 1)
                    if beyond(t, 2):
                        act.wait_ge(soft, t - 1)
                    act.activation(expd[:, r, :], shifted[:, r, :], ACT.Exp, scale=HD ** -0.5).then_inc(exp_done, 1)
                if live(kk, u, L_OT, NT, U):
                    g, t, q = lagged(kk, u, L_OT, U)
                    r = q % 2
                    act.wait_ge(ot_done, t + 1)
                    if beyond(t, 2):
                        act.wait_ge(fc_done, t - 1)
                    act.activation(o_t[:, r, :], ps[5][:, 0:TILE], ACT.Copy).then_inc(ot_sb, 1)
                if live(kk, u, L_BACK, NT, U):
                    g, t, q = lagged(kk, u, L_BACK, U)
                    r = q % 2
                    act.wait_ge(back_done, t + 1)
                    act.activation(k.xt[:, bass.ds(t * TILE, TILE)], ps[7][:, 0:TILE], ACT.Copy).then_inc(xt_done, 1)
            steps(act, NT, DEPTH, step, U, ring=4)

        @block.vector
        def _(dve):
            def step(kk, u):
                if live(kk, u, L_PVP, NT, U):
                    g, t, q = lagged(kk, u, L_PVP, U)
                    r = q % 2
                    dve.wait_ge(exp_done, t + 1)
                    if beyond(t, 2):
                        dve.wait_ge(half_done, t - 1)
                    e = expd[:, r, :].rearrange("p (h t) -> p t h", h=HEADS)
                    v = qkv[:, q, 2 * D:3 * D].rearrange("p (t d) -> p t d", d=HD)
                    dve.tensor_tensor(pv[:, r, :, :].rearrange("p t (h d) -> p t h d", d=HD),
                                      e.unsqueeze(3).to_broadcast([P, HEADS, HEADS, HD]),
                                      v.unsqueeze(2).to_broadcast([P, HEADS, HEADS, HD]), ALU.mult).then_inc(pvp_done, 1)
                    if beyond(t, 2):
                        dve.wait_ge(rden_done, t - 1)
                    dve.tensor_reduce(den[:, r, :], expd[:, r, :].rearrange("p (h t) -> p h t", h=HEADS),
                                      AX.X, ALU.add).then_inc(soft, 1)
                if live(kk, u, L_NORM, NT, U):
                    g, t, q = lagged(kk, u, L_NORM, U)
                    r = q % 2
                    dve.wait_ge(pv_done, t + 1)
                    dve.wait_ge(rden_done, t + 1)
                    if beyond(t, 2):
                        dve.wait_ge(ot_done, t - 1)
                    dve.tensor_tensor(o_nat[:, r, :].rearrange("p (h d) -> p h d", d=HD),
                                      ps[4][:, 0:D].rearrange("p (h d) -> p h d", d=HD),
                                      rden[:, r, :].unsqueeze(2).to_broadcast([P, HEADS, HD]), ALU.mult).then_inc(norm_done, 1)
                if live(kk, u, L_LN, NT, U):
                    g, t, q = lagged(kk, u, L_LN, U)
                    r = q % 2
                    dve.wait_ge(fc_done, t + 1)
                    dve.wait_ge(r_here[q], g * 16 + 16)
                    if beyond(t, 2):
                        dve.wait_ge(xn_done, t - 1)
                    dve.tensor_tensor(y[:, r, :], ps[6][:, 0:D], x_res[:, q, :], ALU.add).then_inc(dsem, 1)
                    dve.wait_ge(dsem, t * 2 + 1)
                    dve.bn_stats(st[:, r, :], y[:, r, :]).then_inc(dsem, 1)
                if live(kk, u, L_PVP, NT, U):
                    g, t, q = lagged(kk, u, L_PVP, U)
                    r = q % 2
                    dve.wait_ge(soft, t + 1)
                    if beyond(t, 2):
                        dve.wait_ge(norm_done, t - 1)
                    dve.reciprocal(rden[:, r, :], den[:, r, :]).then_inc(rden_done, 1)
                if live(kk, u, L_XN, NT, U):
                    g, t, q = lagged(kk, u, L_XN, U)
                    r = q % 2
                    dve.wait_ge(rstd_done, t + 1)
                    if beyond(t, 2):
                        dve.wait_ge(back_done, t - 1)
                    if live(kk, u, L_LN, NT, U):
                        dve.wait_ge(dsem, lagged(kk, u, L_LN, U)[1] * 2 + 2)
                    dve.tensor_scalar(xn[:, r, :], y[:, r, :], mv[:, r, 0:1], rstd[:, r, :], ALU.subtract, ALU.mult).then_inc(xn_done, 1)
                if live(kk, u, L_SC, NT, U):
                    g, t, q = lagged(kk, u, L_SC, U)
                    r = q % 2
                    dve.wait_ge(score_done, t + 1)
                    sc = ps[2 + r][:, 0:256].rearrange("p (h t) -> p h t", h=HEADS)
                    dve.tensor_reduce(top[:, r, :], sc, AX.X, ALU.max).then_inc(topped, 1)
                if live(kk, u, L_LN, NT, U):
                    g, t, q = lagged(kk, u, L_LN, U)
                    r = q % 2
                    if not live(kk, u, L_XN, NT, U):
                        dve.wait_ge(dsem, t * 2 + 2)
                    dve.bn_aggr(mv[:, r, :], st[:, r, :]).then_inc(stat_done, 1)
                if live(kk, u, L_SC, NT, U):
                    g, t, q = lagged(kk, u, L_SC, U)
                    r = q % 2
                    dve.wait_ge(topped, t + 1)
                    if beyond(t, 2):
                        dve.wait_ge(exp_done, t - 1)
                    sc = ps[2 + r][:, 0:256].rearrange("p (h t) -> p h t", h=HEADS)
                    dve.tensor_tensor(shifted[:, r, :].rearrange("p (h t) -> p h t", h=HEADS), sc,
                                      top[:, r, :].unsqueeze(2).to_broadcast([P, HEADS, HEADS]), ALU.subtract).then_inc(shift_done, 1)
                if live(kk, u, L_QK, NT, U):
                    g, t, q = lagged(kk, u, L_QK, U)
                    r = q % 2
                    dve.wait_ge(qkv_sb, t + 1)
                    if beyond(t, 2):
                        dve.wait_ge(score_done, t - 1)
                    qx = qkv[:, q, 0:D].rearrange("p (h d) -> p d h", d=HD)
                    kx = qkv[:, q, D:2 * D].rearrange("p (t d) -> p d t", d=HD)
                    dve.tensor_tensor(prod[:, r, :, :].rearrange("p d (h t) -> p d h t", h=HEADS),
                                      qx.unsqueeze(3).to_broadcast([P, HD, HEADS, HEADS]),
                                      kx.unsqueeze(2).to_broadcast([P, HD, HEADS, HEADS]), ALU.mult).then_inc(prod_done, 1)
            steps(dve, NT, DEPTH, step, U, ring=4)

        @block.gpsimd
        def _(pool):
            def step(kk, u):
                if live(kk, u, L_PVP, NT, U):
                    g, t, q = lagged(kk, u, L_PVP, U)
                    r = q % 2
                    pool.wait_ge(pvp_done, t + 1)
                    if beyond(t, 2):
                        pool.wait_ge(pv_done, t - 1)
                    h = HEADS // 2
                    pool.tensor_tensor(pvh[:, r, :, :], pv[:, r, 0:h, :], pv[:, r, h:2 * h, :], ALU.add).then_inc(half_done, 1)
                if live(kk, u, L_LN, NT, U):
                    g, t, q = lagged(kk, u, L_LN, U)
                    r = q % 2
                    pool.wait_ge(stat_done, t + 1)
                    if beyond(t, 2):
                        pool.wait_ge(xn_done, t - 1)
                    pool.tensor_tensor(var[:, r, :], mv[:, r, 1:2], k.eps5[:, 0:1], ALU.add).then_inc(var_done, 1)
                    pool.wait_ge(var_done, t + 1)
                    pool.tensor_tensor(rstd[:, r, :], var[:, r, :], k.mhalf[:, 0:1], ALU.pow).then_inc(rstd_done, 1)
            steps(pool, NT, DEPTH, step, U, ring=4)



class Norm:

    def __init__(self, nc, ctx, sem, name, fwd_bank, back_bank, eps, xn=None, ring=2):
        sb = lambda n, s: ctx.enter_context(nc.sbuf_tensor(f"{name}_{n}", s, F32))
        self.fwd, self.back, self.eps, self.ring = fwd_bank, back_bank, eps, ring
        self.mark, self.y = sb("mark", [P, 1]), sb("y", [P, 2, CH])
        self.st, self.mv = sb("st", [P, TPC, 6]), sb("mv", [P, TPC, 2])
        self.var, self.rstd = sb("var", [P, TPC]), sb("rstd", [P, 2, TPC])
        self.xn = sb("xn", [P, 2, TPC, D]) if xn is None else xn
        self.y_ready, self.fwd_done, self.stat_done, self.aggr_done, self.var_done, self.rstd_done, \
            self.xn_done, self.back_done = (sem(f"{name[2:]}_{n}") for n in (
                "y_ready", "fwd_done", "stat_done", "aggr_done", "var_done", "rstd_done", "xn_done", "back_done"))


def wait_older(eng, sem, n, ago):
    if beyond(n, ago):
        eng.wait_ge(sem, n - ago + 1)


def norm_fwd(pe, k, L, n, c):
    pe.wait_ge(L.y_ready, n + 1)
    wait_older(pe, L.xn_done, n, 1)
    for j in range(TPC):
        mm = pe.transpose(L.fwd[:, j * D:(j + 1) * D], L.y[:, c % 2, j * D:(j + 1) * D], k.ident[:])
    mm.then_inc(L.fwd_done, 1)


def norm_stats(dve, k, L, n, c):
    dve.wait_ge(L.fwd_done, n + 1)
    for j in range(TPC):
        st = dve.bn_stats(L.st[:, j, :], L.fwd[:, j * D:(j + 1) * D])
    st.then_inc(L.stat_done, 1)
    dve.wait_ge(L.stat_done, n + 1)
    dve.tensor_copy(L.mark[:], L.st[:, 0, 0:1])
    for j in range(TPC):
        ag = dve.bn_aggr(L.mv[:, j, :], L.st[:, j, :])
    ag.then_inc(L.aggr_done, 1)


def norm_rstd(pool, k, L, n, c):
    pool.wait_ge(L.aggr_done, n + 1)
    pool.tensor_tensor(L.var[:], L.mv[:, :, 1], L.eps[:], ALU.add).then_inc(L.var_done, 1)
    pool.wait_ge(L.var_done, n + 1)
    pool.tensor_tensor(L.rstd[:, c % 2, :], L.var[:], k.mhalf[:], ALU.pow).then_inc(L.rstd_done, 1)


def norm_apply(dve, k, L, n, c):
    dve.wait_ge(L.rstd_done, n + 1)
    wait_older(dve, L.back_done, n, L.ring)
    for j in range(TPC):
        ts = dve.tensor_scalar(L.xn[:, c % L.ring, j, :], L.fwd[:, j * D:(j + 1) * D], L.mv[:, j, 0:1],
                               L.rstd[:, c % 2, j:j + 1], ALU.subtract, ALU.mult)
    ts.then_inc(L.xn_done, 1)


def norm_back(pe, k, L, n, c):
    pe.wait_ge(L.xn_done, n + 1)
    for j in range(TPC):
        mm = pe.transpose(L.back[:, j * D:(j + 1) * D], L.xn[:, c % L.ring, j, :], k.ident[:])
    mm.then_inc(L.back_done, 1)


def stage_b(nc, k, a):
    with ExitStack() as ctx:
        sb = lambda n, s, t=F32: ctx.enter_context(nc.sbuf_tensor("b_" + n, s, t))
        sem = cleared_later(nc, ctx, "b_")
        w = sb("w", [P, 3 * HIDDEN])
        sg, h = sb("sg", [P, 2, CH]), sb("h", [P, 2, NJ, CH])
        w_done = sem("w_done")
        gate_done, up_done, silu_done, h_done, down_done = map(sem, "gate_done up_done silu_done h_done down_done".split())
        copied = sem("copied")
        ps = k.ps
        L = Norm(nc, ctx, sem, "b_ln", ps[5], ps[6], k.eps5)
        out_done = k.x_ready
        block = ctx.enter_context(nc.Block())
        DEPTH = 4
        at = lambda c: slice(c * CH, (c + 1) * CH)

        @block.sync
        def _(sp):
            for to, w, cols, here in block_pieces(k, a):
                sp.dma_start(to[:], w[0:P, cols]).then_inc(here, 16)

        @block.tensor
        def _(pe):
            pe.wait_ge(w_done, 1)
            for s in range(NC + DEPTH):
                if s < NC:
                    for j in range(NJ):
                        m = NJ * s + j
                        if m >= 2:
                            pe.wait_ge(silu_done, m - 1)
                        pe.matmul(ps[m % 2][:], w[:, j * P:(j + 1) * P], k.xt[:, at(s)], start=True, stop=True).then_inc(gate_done, 1)
                        if m >= 2:
                            pe.wait_ge(h_done, m - 1)
                        pe.matmul(ps[2 + m % 2][:], w[:, HIDDEN + j * P:HIDDEN + (j + 1) * P], k.xt[:, at(s)],
                                  start=True, stop=True).then_inc(up_done, 1)
                if 0 <= s - 2 < NC:
                    norm_fwd(pe, k, L, s - 2, s - 2)
                if 0 <= s - 1 < NC:
                    c = s - 1
                    if c >= 1:
                        pe.wait_ge(L.y_ready, c)
                    for j in range(NJ):
                        pe.wait_ge(h_done, NJ * c + j + 1)
                        mm = pe.matmul(ps[4][:], w[:, 2 * HIDDEN + j * P:2 * HIDDEN + (j + 1) * P], h[:, c % 2, j, :],
                                       start=j == 0, stop=j == NJ - 1)
                    mm.then_inc(down_done, 1)
                if 0 <= s - 3 < NC:
                    wait_older(pe, out_done, s - 3, 1)
                    norm_back(pe, k, L, s - 3, s - 3)

        @block.scalar
        def _(act):
            for s in range(NC + DEPTH):
                if s < NC:
                    for j in range(NJ):
                        m = NJ * s + j
                        act.wait_ge(gate_done, m + 1)
                        if m >= 2:
                            act.wait_ge(h_done, m - 1)
                        act.activation(sg[:, m % 2, :], ps[m % 2][:], ACT.Silu).then_inc(silu_done, 1)
                if 0 <= s - 3 < NC:
                    c = s - 3
                    act.wait_ge(L.back_done, c + 1)
                    act.activation(k.xt[:, at(c)], L.back[:], ACT.Copy).then_inc(out_done, 1)

        @block.vector
        def _(dve):
            dve.wait_ge(k.wffn_in, 16)
            dve.tensor_scalar(w[:], k.wffn[:], 1.0 / 127.0, None, ALU.mult).then_inc(w_done, 1)
            for s in range(NC + DEPTH):
                if 0 <= s - 3 < NC:
                    norm_apply(dve, k, L, s - 3, s - 3)
                if s < NC:
                    for j in range(NJ):
                        m = NJ * s + j
                        dve.wait_ge(silu_done, m + 1)
                        dve.wait_ge(up_done, m + 1)
                        if s >= 2:
                            dve.wait_ge(down_done, s - 1)
                        dve.tensor_tensor(h[:, s % 2, j, :], sg[:, m % 2, :], ps[2 + m % 2][:], ALU.mult).then_inc(h_done, 1)
                if 0 <= s - 2 < NC:
                    norm_stats(dve, k, L, s - 2, s - 2)
                if 0 <= s - 1 < NC:
                    c = s - 1
                    dve.wait_ge(down_done, c + 1)
                    if c >= 2:
                        dve.wait_ge(L.fwd_done, c - 1)
                    dve.tensor_tensor(L.y[:, c % 2, :], ps[4][:], k.xt[:, at(c)], ALU.add).then_inc(L.y_ready, 1)

        @block.gpsimd
        def _(pool):
            for s in range(NC + DEPTH):
                if 0 <= s - 2 < NC:
                    norm_rstd(pool, k, L, s - 2, s - 2)
                if 0 <= s - 4 < NC:
                    c = s - 4
                    pool.wait_ge(out_done, c + 1)
                    pool.tensor_copy(k.xt0[:, at(c)], k.xt[:, at(c)]).then_inc(copied, 1)


def block_pieces(k, a):
    return ((k.wqkv, a["w1"], slice(0, W1COLS), k.wqkv_in), (k.wo, a["w2"], slice(0, O_LN1), k.wo_in),
            (k.ln1, a["w2"], slice(O_LN1, O_F1), k.ln1_in),
            (k.wf1, a["w2"], slice(O_F1, O_F2), k.wf1_in), (k.wf2, a["w2"], slice(O_F2, O_LN2), k.wf2_in),
            (k.ln2, a["w2"], slice(O_LN2, W2COLS), k.ln2_in))


def stage_c(nc, k, a):
    N = BLOCKS * NC
    with ExitStack() as ctx:
        sb = lambda n, s, t=F32: ctx.enter_context(nc.sbuf_tensor("c_" + n, s, t))
        sem = cleared_later(nc, ctx, "c_")
        wqkv, wo, wf1, wf2, ln1, ln2 = k.wqkv, k.wo, k.wf1, k.wf2, k.ln1, k.ln2
        b1p = sb("b1p", [P, 2])
        eq, ek = sb("eq", [P, CH]), sb("ek", [P, CH])
        qf, kf, kv = sb("qf", [P, 2, CH]), sb("kf", [P, CH]), sb("kv", [P, CH])
        ksum, kvsum = sb("ksum", [P, NC]), sb("kvsum", [P, NC])
        lz, z, qz = sb("lz", [P, CH]), sb("z", [P, CH]), sb("qz", [P, 2, CH])
        wo_kv = sb("wo_kv", [P, 2, D])
        g1, g2, h = sb("g1", [P, CH]), sb("g2", [P, CH]), sb("h", [P, 2, NF, CH])
        wqkv_in, wo_in, wf1_in, wf2_in, ln1_in, ln2_in = k.wqkv_in, k.wo_in, k.wf1_in, k.wf2_in, k.ln1_in, k.ln2_in
        cleared = sem("cleared")
        (b1p_done, q_done, k_done, v_done, eq_done, ek_done, eqadd_done, eqmin_done, ekmin_done, qf_done, kf_done, kv_done,
         lz_done, z_done, qz_done, wokv_done, wo_done, g1_done, x1_done, hp_done, hg_done, w2_done, g2_done) = map(
            sem, "b1p_done q_done k_done v_done eq_done ek_done eqadd_done eqmin_done ekmin_done qf_done kf_done kv_done "
                 "lz_done z_done qz_done wokv_done wo_done g1_done x1_done hp_done hg_done w2_done g2_done".split())
        x_ready = k.x_ready
        contrib = k.contrib.rearrange("(p r) d -> p (r d)", p=P)
        b_q, b_k, b_v, b_g, b_h, b_fwd, b_back = k.ps[0], k.ps[1], k.ps[2], k.ps[3], k.ps[4:6], k.ps[6], k.ps[7]
        L1 = Norm(nc, ctx, sem, "c_ln1", b_fwd, b_back, k.eps6)
        L2 = Norm(nc, ctx, sem, "c_ln2", b_fwd, b_back, k.eps6)
        block = ctx.enter_context(nc.Block())
        at = lambda c: slice(c * CH, (c + 1) * CH)
        A_WO, A_N1, A_W1, A_W2, A_N2 = 1, 2, 3, 4, 5
        DEPTH = A_N2

        def done(eng, sem, kk, u, lag, per=1):
            if live(kk, u, lag, N, NC):
                eng.wait_ge(sem, (lagged(kk, u, lag, NC)[1] + 1) * per)

        def items(eng, body):
            steps(eng, N, DEPTH, body, NC, ring=2)

        @block.sync
        def _(sp):
            def clear(kk):
                for i in range(2):
                    sp.dma_start(contrib[:, bass.ds(kk * 4096 + i * 2048, 2048)], k.zeros[:]).then_inc(cleared, 16)
            clear(0)
            with sp.Fori(1, BLOCKS) as kk:
                over = ((kv_done, NC * kk), (g1_done, NC * kk), (x1_done, NC * kk), (hg_done, NC * NF * kk), (g2_done, NC * kk), (x_ready, NC * kk + NC))
                for (to, w, cols, here), (used, count) in zip(block_pieces(k, a), over):
                    sp.wait_ge(used, count)
                    sp.dma_start(to[:], w[bass.ds(kk * P, P), cols]).then_inc(here, 16)
                clear(kk)
            sp.dma_start(k.ws[:], a["ws"]).then_inc(k.ws_in, 16)
            sp.dma_start(k.wsd[:], a["wsd"]).then_inc(k.ws_in, 16)
            sp.wait_ge(cleared, BLOCKS * 32)

        @block.tensor
        def _(pe):
            def step(kk, u):
                if live(kk, u, A_N1, N, NC):
                    g, n, c = lagged(kk, u, A_N1, NC)
                    done(pe, L2.xn_done, kk, u, A_N2 + 1)
                    norm_fwd(pe, k, L1, n, c)
                if live(kk, u, 0, N, NC):
                    g, n, c = lagged(kk, u, 0, NC)
                    if c == 0:
                        pe.wait_ge(wqkv_in, g * 16 + 16)
                    pe.wait_ge(x_ready, n + 1)
                    done(pe, qf_done, kk, u, 1)
                    pe.matmul(b_q[:], wqkv[:, 0:D], k.xt[:, at(c)], start=True, stop=True).then_inc(q_done, 1)
                    done(pe, kf_done, kk, u, 1)
                    pe.matmul(b_k[:], wqkv[:, D:2 * D], k.xt[:, at(c)], start=True, stop=True).then_inc(k_done, 1)
                    done(pe, kv_done, kk, u, 1)
                    pe.matmul(b_v[:], wqkv[:, 2 * D:3 * D], k.xt[:, at(c)], start=True, stop=True).then_inc(v_done, 1)
                if live(kk, u, A_W2, N, NC):
                    g, n, c = lagged(kk, u, A_W2, NC)
                    if c == 0:
                        pe.wait_ge(wf2_in, g * 16 + 16)
                    done(pe, g1_done, kk, u, A_WO + 1)
                    for j in range(NF):
                        pe.wait_ge(hg_done, n * NF + j + 1)
                        mm = pe.matmul(b_g[:], wf2[:, j * D:(j + 1) * D], h[:, c % 2, j, :], start=j == 0, stop=j == NF - 1)
                    mm.then_inc(w2_done, 1)
                if live(kk, u, A_N2, N, NC):
                    g, n, c = lagged(kk, u, A_N2, NC)
                    done(pe, L1.xn_done, kk, u, A_N1)
                    norm_fwd(pe, k, L2, n, c)
                if live(kk, u, A_N1, N, NC):
                    g, n, c = lagged(kk, u, A_N1, NC)
                    if live(kk, u, A_N2 + 1, N, NC):
                        pe.wait_ge(x_ready, lagged(kk, u, A_N2 + 1, NC)[1] + NC + 1)
                    norm_back(pe, k, L1, n, c)
                if live(kk, u, A_WO, N, NC):
                    g, n, c = lagged(kk, u, A_WO, NC)
                    pe.wait_ge(wokv_done, n + 1)
                    pe.wait_ge(qz_done, n + 1)
                    done(pe, g2_done, kk, u, A_W2)
                    pe.matmul(b_g[:], wo_kv[:, c % 2, :], qz[:, c % 2, :], start=True, stop=True).then_inc(wo_done, 1)
                if live(kk, u, A_W1, N, NC):
                    g, n, c = lagged(kk, u, A_W1, NC)
                    if c == 0:
                        pe.wait_ge(wf1_in, g * 16 + 16)
                    pe.wait_ge(x1_done, n + 1)
                    for j in range(NF):
                        if j >= 2:
                            pe.wait_ge(hg_done, n * NF + j - 1)
                        elif beyond(n, 1):
                            pe.wait_ge(hg_done, n * NF + j - 1)
                        pe.matmul(b_h[j % 2][:], wf1[:, j * P:(j + 1) * P], k.xt[:, at(c)], start=True, stop=True).then_inc(hp_done, 1)
                if live(kk, u, A_N2, N, NC):
                    g, n, c = lagged(kk, u, A_N2, NC)
                    done(pe, x1_done, kk, u, A_N1)
                    if not live(kk, u, A_N1, N, NC):
                        pe.wait_ge(x_ready, n + NC)
                    norm_back(pe, k, L2, n, c)
            items(pe, step)

        @block.scalar
        def _(act):
            def step(kk, u):
                act.preload_act_table_set(EXP_LN_SET)
                if live(kk, u, 0, N, NC):
                    g, n, c = lagged(kk, u, 0, NC)
                    act.wait_ge(q_done, n + 1)
                    done(act, qf_done, kk, u, 1)
                    act.activation(eq[:], b_q[:], ACT.Exp, bias=wqkv[:, 3 * D:3 * D + 1]).then_inc(eq_done, 1)
                    act.wait_ge(k_done, n + 1)
                    done(act, kf_done, kk, u, 1)
                    act.activation(ek[:], b_k[:], ACT.Exp, bias=wqkv[:, 3 * D + 1:3 * D + 2]).then_inc(ek_done, 1)
                if live(kk, u, A_WO, N, NC):
                    g, n, c = lagged(kk, u, A_WO, NC)
                    act.wait_ge(kf_done, n + 1)
                    act.wait_ge(qf_done, n + 1)
                    act.activation(lz[:], qf[:, c % 2, :], ACT.Ln, bias=k.eps6[:, 0:1], scale=ksum[:, c:c + 1]).then_inc(lz_done, 1)
                    act.wait_ge(lz_done, n + 1)
                    done(act, qz_done, kk, u, A_WO + 1)
                    act.activation(z[:], lz[:], ACT.Exp, scale=-1.0).then_inc(z_done, 1)
                act.preload_act_table_set(GELU_SET)
                if live(kk, u, A_W2, N, NC):
                    g, n, c = lagged(kk, u, A_W2, NC)
                    act.wait_ge(w2_done, n + 1)
                    done(act, L2.y_ready, kk, u, A_W2 + 1)
                    act.activation(g2[:], b_g[:], ACT.Gelu_apprx_tanh, bias=wf2[:, NF * D:NF * D + 1]).then_inc(g2_done, 1)
                if live(kk, u, A_WO, N, NC):
                    g, n, c = lagged(kk, u, A_WO, NC)
                    act.wait_ge(wo_done, n + 1)
                    done(act, L1.y_ready, kk, u, A_WO + 1)
                    act.activation(g1[:], b_g[:], ACT.Gelu_apprx_tanh, bias=wo[:, D:D + 1]).then_inc(g1_done, 1)
                if live(kk, u, A_W1, N, NC):
                    g, n, c = lagged(kk, u, A_W1, NC)
                    done(act, w2_done, kk, u, A_W1 + 2)
                    for j in range(NF):
                        act.wait_ge(hp_done, n * NF + j + 1)
                        act.activation(h[:, c % 2, j, :], b_h[j % 2][:], ACT.Gelu_apprx_tanh, bias=wf1[:, FF + j:FF + j + 1]).then_inc(hg_done, 1)
                if live(kk, u, A_N2, N, NC):
                    g, n, c = lagged(kk, u, A_N2, NC)
                    if c == 0:
                        act.wait_ge(ln2_in, g * 16 + 16)
                    act.wait_ge(L2.back_done, n + 1)
                    act.activation(k.xt[:, at(c)], b_back[:], ACT.Identity, bias=ln2[:, 1:2], scale=ln2[:, 0:1]).then_inc(x_ready, 1)
            items(act, step)

        @block.vector
        def _(dve):
            def step(kk, u):
                if live(kk, u, A_N1, N, NC):
                    g, n, c = lagged(kk, u, A_N1, NC)
                    norm_stats(dve, k, L1, n, c)
                if live(kk, u, A_WO, N, NC):
                    g, n, c = lagged(kk, u, A_WO, NC)
                    if c == 0:
                        dve.wait_ge(wo_in, g * 16 + 16)
                    dve.wait_ge(kv_done, n + 1)
                    done(dve, wo_done, kk, u, A_WO + 2)
                    dve.tensor_scalar(wo_kv[:, c % 2, :], wo[:, 0:D], kvsum[:, c:c + 1], None, ALU.mult).then_inc(wokv_done, 1)
                if live(kk, u, 0, N, NC):
                    g, n, c = lagged(kk, u, 0, NC)
                    if c == 0:
                        dve.wait_ge(wqkv_in, g * 16 + 16)
                        dve.tensor_scalar(b1p[:], wqkv[:, 3 * D:3 * D + 2], 1.0, None, ALU.add).then_inc(b1p_done, 1)
                    dve.wait_ge(eq_done, n + 1)
                    dve.tensor_scalar(eq[:], eq[:], 1.0, -1.0, ALU.min, ALU.add).then_inc(eqmin_done, 1)
                    dve.wait_ge(eqmin_done, n + 1)
                    dve.tensor_scalar(eq[:], eq[:], 1.0, None, ALU.add).then_inc(eqadd_done, 1)
                if live(kk, u, A_N1, N, NC):
                    g, n, c = lagged(kk, u, A_N1, NC)
                    norm_apply(dve, k, L1, n, c)
                if live(kk, u, 0, N, NC):
                    g, n, c = lagged(kk, u, 0, NC)
                    dve.wait_ge(ek_done, n + 1)
                    dve.tensor_scalar(ek[:], ek[:], 1.0, None, ALU.min).then_inc(ekmin_done, 1)
                    dve.wait_ge(eqadd_done, n + 1)
                    if c == 0:
                        dve.wait_ge(b1p_done, g + 1)
                    done(dve, qz_done, kk, u, 2)
                    dve.scalar_tensor_tensor(qf[:, c % 2, :], b_q[:], b1p[:, 0:1], eq[:], ALU.add, ALU.max).then_inc(qf_done, 1)
                    dve.wait_ge(ekmin_done, n + 1)
                    dve.scalar_tensor_tensor(kf[:], b_k[:], b1p[:, 1:2], ek[:], ALU.add, ALU.max,
                                             accum_out=ksum[:, c:c + 1]).then_inc(kf_done, 1)
                    dve.wait_ge(kf_done, n + 1)
                    dve.wait_ge(v_done, n + 1)
                    dve.scalar_tensor_tensor(kv[:], b_v[:], wqkv[:, 3 * D + 2:3 * D + 3], kf[:], ALU.add, ALU.mult,
                                             accum_out=kvsum[:, c:c + 1]).then_inc(kv_done, 1)
                if live(kk, u, A_N2, N, NC):
                    g, n, c = lagged(kk, u, A_N2, NC)
                    norm_stats(dve, k, L2, n, c)
                if live(kk, u, A_N1, N, NC):
                    g, n, c = lagged(kk, u, A_N1, NC)
                    if c == 0:
                        dve.wait_ge(ln1_in, g * 16 + 16)
                    dve.wait_ge(L1.back_done, n + 1)
                    dve.tensor_scalar(k.xt[:, at(c)], b_back[:], ln1[:, 0:1], ln1[:, 1:2],
                                      ALU.mult, ALU.add).then_inc(x1_done, 1)
                if live(kk, u, A_N2, N, NC):
                    g, n, c = lagged(kk, u, A_N2, NC)
                    norm_apply(dve, k, L2, n, c)
            items(dve, step)

        @block.gpsimd
        def _(pool):
            def step(kk, u):
                if live(kk, u, A_N1, N, NC):
                    g, n, c = lagged(kk, u, A_N1, NC)
                    norm_rstd(pool, k, L1, n, c)
                if live(kk, u, A_WO, N, NC):
                    g, n, c = lagged(kk, u, A_WO, NC)
                    pool.wait_ge(z_done, n + 1)
                    done(pool, wo_done, kk, u, A_WO + 2)
                    pool.tensor_tensor(qz[:, c % 2, :], qf[:, c % 2, :], z[:], ALU.mult).then_inc(qz_done, 1)
                if live(kk, u, A_W2, N, NC):
                    g, n, c = lagged(kk, u, A_W2, NC)
                    pool.wait_ge(g2_done, n + 1)
                    done(pool, L2.fwd_done, kk, u, A_W2 + 2)
                    pool.tensor_tensor(L2.y[:, c % 2, :], g2[:], k.xt[:, at(c)], ALU.add).then_inc(L2.y_ready, 1)
                if live(kk, u, A_N2, N, NC):
                    g, n, c = lagged(kk, u, A_N2, NC)
                    norm_rstd(pool, k, L2, n, c)
                if live(kk, u, A_WO, N, NC):
                    g, n, c = lagged(kk, u, A_WO, NC)
                    pool.wait_ge(g1_done, n + 1)
                    done(pool, L1.fwd_done, kk, u, A_WO + 2)
                    pool.tensor_tensor(L1.y[:, c % 2, :], g1[:], k.xt[:, at(c)], ALU.add).then_inc(L1.y_ready, 1)
            items(pool, step)


def stage_d_route(nc, k, a):
    with ExitStack() as ctx:
        sb = lambda n, s, t=F32: ctx.enter_context(nc.sbuf_tensor("d_" + n, s, t))
        sem = cleared_later(nc, ctx, "d_")
        FAR = 8192.0
        row = sb("row", [P, 4, TPC, ROW])
        zt = sb("zt", [P, 2, CH])
        lg, sh, ex, em = (sb(n, [P, 2, TPC, E]) for n in ("lg", "sh", "ex", "em"))
        rest_, mask = sb("rest", [P, TPC, E]), sb("mask", [P, 2, TPC, E])
        maskb, macc = sb("maskb", [P, 2, TPC, E], BF16), sb("macc", [P, 2, E], BF16)
        msum = sb("msum", [P, E])
        m8, den, rden = sb("m8", [P, TPC, 8]), sb("den", [P, TPC]), sb("rden", [P, TPC])
        far, place = sb("far", [P, TPC, E]), sb("place", [P, 2, TPC, E], BF16)
        hot = sb("hot", [P, TPC, PAIRS * P], BF16)
        sg, hs = sb("sg", [FE, CH]), sb("hs", [FE, 2, CH])
        scan, scan_done = sb("scan", [P, TPC * E]), sem("scan_done")
        onesf = sb("onesf", [P, TPC * E])
        pay = sb("pay", [P, NT, 4], BF16)
        ps = k.ps
        L = Norm(nc, ctx, sem, "d_ln", ps[5], ps[6], k.eps5, xn=row[:, :, :, 0:D], ring=4)
        rows_out = [sem(f"rows_out{i}") for i in range(4)]
        (init, zt_done, lg_done, lgc_done, gate_done, up_done, silu_done, hs_done, down_done, base_done, top_done,
         sh_done, rep_done, ex_done, mask_done, em_done, den_done, rden_done, row_done, maskb_done, macc_done,
         msum_done, pos_done, far_done, place_done, hot_done, tab_done, pay_done) = map(
            sem, "init zt_done lg_done lgc_done gate_done up_done silu_done hs_done down_done base_done top_done "
                 "sh_done rep_done ex_done mask_done em_done den_done rden_done row_done maskb_done macc_done "
                 "msum_done pos_done far_done place_done hot_done tab_done pay_done".split())
        block = ctx.enter_context(nc.Block())
        at = lambda c: slice(c * CH, (c + 1) * CH)
        STEPS = NC + 6

        @block.sync
        def _(sp):
            for c in range(NC):
                sp.wait_ge(row_done, 2 * c + 2)
                sp.dma_start(k.rows[c * CH:(c + 1) * CH, :].rearrange("(j p) w -> p j w", p=P), row[:, c % 4, :, :])\
                    .then_inc(rows_out[c % 4], 16)
            for i in range(4):
                sp.wait_ge(rows_out[i], 16 * (NC // 4))

        @block.tensor
        def _(pe):
            pe.wait_ge(k.ws_in, 32)
            for s in range(STEPS):
                c = s
                if c < NC:
                    norm_fwd(pe, k, L, c, c)
                c = s - 2
                if 0 <= c < NC:
                    pe.wait_ge(zt_done, c + 1)
                    if c >= 1:
                        pe.wait_ge(lgc_done, c)
                    for j in range(TPC):
                        mm = pe.matmul(ps[0][:, j * E:(j + 1) * E], zt[:, c % 2, j * P:(j + 1) * P], k.ws[:, 0:E], start=True, stop=True)
                    mm.then_inc(lg_done, 1)
                    if c >= 1:
                        pe.wait_ge(hs_done, c)
                    pe.matmul(ps[1][0:FE, :], k.ws[:, E:E + FE], zt[:, c % 2, :], start=True, stop=True).then_inc(gate_done, 1)
                    pe.matmul(ps[2][0:FE, :], k.ws[:, E + FE:E + 2 * FE], zt[:, c % 2, :], start=True, stop=True).then_inc(up_done, 1)
                c = s - 1
                if 0 <= c < NC:
                    wait_older(pe, zt_done, c, 1)
                    norm_back(pe, k, L, c, c)
                c = s - 3
                if 0 <= c < NC:
                    pe.wait_ge(hs_done, c + 1)
                    if c >= 1:
                        pe.wait_ge(base_done, c)
                    for j in range(TPC):
                        pe.matmul(ps[3][:, j * D:(j + 1) * D], hs[:, c % 2, j * P:(j + 1) * P], k.wsd[:], start=True, stop=False)
                        mm = pe.matmul(ps[3][:, j * D:(j + 1) * D], k.ident[:], row[:, c % 4, j, 0:D], start=False, stop=True)
                    mm.then_inc(down_done, 1)
                c = s - 4
                if 0 <= c < NC:
                    pe.wait_ge(maskb_done, c + 1)
                    if c >= 1:
                        pe.wait_ge(macc_done, c)
                        pe.wait_ge(far_done, c)
                    for j in range(TPC):
                        terms = [(k.tri, maskb[:, c % 2, j, :])] + [(k.ones, maskb[:, c % 2, i, :]) for i in range(j)]
                        if c >= 1:
                            terms.append((k.ones, macc[:, c % 2, :]))
                        for i, (m, v) in enumerate(terms):
                            mm = pe.matmul(ps[4][:, j * E:(j + 1) * E], m[:], v, start=i == 0, stop=i == len(terms) - 1)
                    mm.then_inc(pos_done, 1)
                c = s - 5
                if 0 <= c < NC:
                    pe.wait_ge(pay_done, 1)
                    for j in range(TPC):
                        t = c * TPC + j
                        pe.wait_ge(hot_done, t + 1)
                        for g in range(PAIRS):
                            mm = pe.matmul(ps[7][:, 4 * g:4 * g + 4], hot[:, j, g * P:(g + 1) * P], pay[:, t, :],
                                           start=(t == 0 and g == 0), stop=(t == NT - 1), skip_group_check=True)
                        mm.then_inc(tab_done, 1)

        @block.scalar
        def _(act):
            for s in range(STEPS):
                c = s - 2
                if 0 <= c < NC:
                    act.wait_ge(lg_done, c + 1)
                    if c >= 2:
                        act.wait_ge(mask_done, c - 1)
                    act.activation(lg[:, c % 2, :, :], ps[0][:, 0:TPC * E].rearrange("p (j e) -> p j e", e=E), ACT.Copy).then_inc(lgc_done, 1)
                    act.wait_ge(gate_done, c + 1)
                    if c >= 1:
                        act.wait_ge(hs_done, c)
                    act.activation(sg[:], ps[1][0:FE, :], ACT.Silu).then_inc(silu_done, 1)
                c = s - 1
                if 0 <= c < NC:
                    act.wait_ge(L.back_done, c + 1)
                    if c >= 2:
                        act.wait_ge(up_done, c - 1)
                    act.activation(zt[:, c % 2, :], L.back[:], ACT.Copy).then_inc(zt_done, 1)
                c = s - 3
                if 0 <= c < NC:
                    act.wait_ge(sh_done, c + 1)
                    if c >= 2:
                        act.wait_ge(em_done, c - 1)
                    act.activation(ex[:, c % 2, :, :], sh[:, c % 2, :, :], ACT.Exp).then_inc(ex_done, 1)
                    act.wait_ge(down_done, c + 1)
                    act.activation(k.base[:, c * TPC:(c + 1) * TPC, :], ps[3][:].rearrange("p (j d) -> p j d", d=D), ACT.Copy).then_inc(base_done, 1)

        @block.vector
        def _(dve):
            dve.memset(onesf[:], 1.0).then_inc(init, 1)
            dve.wait_ge(init, 1)
            for s in range(STEPS):
                c = s - 1
                if 0 <= c < NC:
                    if c >= 4:
                        dve.wait_ge(rows_out[c % 4], 16 * (c // 4))
                        dve.wait_ge(down_done, c - 3)
                    norm_apply(dve, k, L, c, c)
                c = s - 5
                if 0 <= c < NC:
                    dve.wait_ge(place_done, c + 1)
                    for j in range(TPC):
                        t = c * TPC + j
                        if t >= TPC:
                            dve.wait_ge(tab_done, t - TPC + 1)
                        full = [P, PAIRS, CAP, 2]
                        dve.tensor_tensor(hot[:, j, :].rearrange("p (g c q) -> p g c q", g=PAIRS, q=2),
                                          k.place_of[:].rearrange("p (c q) -> p c q", q=2).unsqueeze(1).to_broadcast(full),
                                          place[:, c % 2, j, :].rearrange("p (g q) -> p g q", q=2).unsqueeze(2).to_broadcast(full),
                                          ALU.is_equal).then_inc(hot_done, 1)
                c = s
                if c < NC:
                    norm_stats(dve, k, L, c, c)
                c = s - 2
                if 0 <= c < NC:
                    dve.wait_ge(silu_done, c + 1)
                    dve.wait_ge(up_done, c + 1)
                    if c >= 2:
                        dve.wait_ge(down_done, c - 1)
                    dve.tensor_tensor(hs[:, c % 2, :], sg[:], ps[2][0:FE, :], ALU.mult).then_inc(hs_done, 1)
                c = s - 3
                if 0 <= c < NC:
                    l = lg[:, c % 2, :, :]
                    dve.wait_ge(lgc_done, c + 1)
                    for j in range(TPC):
                        i = dve.max(m8[:, j, :], l[:, j, :])
                    i.then_inc(top_done, 1)
                    dve.wait_ge(top_done, c + 1)
                    dve.tensor_tensor(sh[:, c % 2, :, :], l, m8[:, :, 0:1].to_broadcast([P, TPC, E]), ALU.subtract).then_inc(sh_done, 1)
                    for j in range(TPC):
                        i = dve.match_replace(rest_[:, j, :], m8[:, j, :], l[:, j, :], -3e38)
                    i.then_inc(rep_done, 1)
                    dve.wait_ge(rep_done, c + 1)
                    if c >= 2:
                        dve.wait_ge(far_done, c - 1)
                    dve.tensor_tensor(mask[:, c % 2, :, :], rest_[:], l, ALU.not_equal).then_inc(mask_done, 1)
                    dve.wait_ge(mask_done, c + 1)
                    if c >= 2:
                        dve.wait_ge(pos_done, c - 1)
                    dve.tensor_copy(maskb[:, c % 2, :, :], mask[:, c % 2, :, :]).then_inc(maskb_done, 1)
                    if c >= 1:
                        dve.wait_ge(row_done, 2 * c)
                    dve.tensor_tensor_scan(scan[:], onesf[:], mask[:, c % 2, :, :].rearrange("p j e -> p (j e)"), 0.0, ALU.mult, ALU.add).then_inc(scan_done, 1)
                    dve.wait_ge(ex_done, c + 1)
                    dve.tensor_tensor(em[:, c % 2, :, :], ex[:, c % 2, :, :], mask[:, c % 2, :, :], ALU.mult).then_inc(em_done, 1)
                    dve.wait_ge(em_done, c + 1)
                    dve.tensor_reduce(den[:], em[:, c % 2, :, :], AX.X, ALU.add).then_inc(den_done, 1)
                    dve.tensor_reduce(msum[:], mask[:, c % 2, :, :].rearrange("p j e -> p e j"), AX.X, ALU.add).then_inc(msum_done, 1)
                    dve.wait_ge(den_done, c + 1)
                    dve.reciprocal(rden[:], den[:]).then_inc(rden_done, 1)
                    dve.wait_ge(msum_done, c + 1)
                    if c >= 1:
                        dve.wait_ge(macc_done, c)
                        dve.wait_ge(pos_done, c)
                        dve.tensor_tensor(macc[:, (c + 1) % 2, :], msum[:], macc[:, c % 2, :], ALU.add).then_inc(macc_done, 1)
                    else:
                        dve.tensor_copy(macc[:, 1, :], msum[:]).then_inc(macc_done, 1)
                c = s - 4
                if 0 <= c < NC:
                    dve.wait_ge(pos_done, c + 1)
                    dve.scalar_tensor_tensor(far[:], mask[:, c % 2, :, :], -FAR, ps[4][:, 0:TPC * E].rearrange("p (j e) -> p j e", e=E),
                                             ALU.mult, ALU.add).then_inc(far_done, 1)
                    dve.wait_ge(far_done, c + 1)
                    dve.tensor_scalar(place[:, c % 2, :, :], far[:], FAR, None, ALU.add).then_inc(place_done, 1)

        @block.gpsimd
        def _(pool):
            for s in range(STEPS):
                c = s
                if c < NC:
                    if c >= 2:
                        pool.wait_ge(L.fwd_done, c - 1)
                    pool.tensor_tensor(L.y[:, c % 2, :], k.xt0[:, at(c)], k.xt[:, at(c)], ALU.add).then_inc(L.y_ready, 1)
                    norm_rstd(pool, k, L, c, c)
                if s < 4:
                    for t in range(s * NT // 4, (s + 1) * NT // 4):
                        pool.memset(pay[:, t, 0:1], float(t))
                        pool.memset(pay[:, t, 3:4], float(t % TPC))
                if s == 3:
                    pool.memset(pay[:, :, 2:3], 1.0)
                    pool.tensor_copy(pay[:, :, 1], k.iota_pf[:].to_broadcast([P, NT])).then_inc(pay_done, 1)
                c = s - 3
                if 0 <= c < NC:
                    pool.wait_ge(L.xn_done, c + 1)
                    pool.wait_ge(scan_done, c + 1)
                    pool.tensor_copy(row[:, c % 4, :, D + E:ROW], scan[:].rearrange("p (j e) -> p j e", e=E)).then_inc(row_done, 1)
                    pool.wait_ge(rden_done, c + 1)
                    pool.tensor_tensor(row[:, c % 4, :, D:D + E], em[:, c % 2, :, :],
                                       rden[:].unsqueeze(2).to_broadcast([P, TPC, E]), ALU.mult).then_inc(row_done, 1)


def stage_d_experts(nc, k, a):
    U = 8
    with ExitStack() as ctx:
        sb = lambda n, s, t=F32: ctx.enter_context(nc.sbuf_tensor("e_" + n, s, t))
        sem = cleared_later(nc, ctx, "e_")
        sems = lambda n: [sem(f"{n}{i}") for i in range(U)]
        tab = sb("tab", [P, PAIRS, 4])
        tok, tok8, none, dest0 = (sb(n, [P, PAIRS]) for n in ("tok", "tok8", "none", "dest0"))
        token = sb("token", [P, PAIRS], I32)
        dest = sb("dest", [P, U, 1], I32)
        got = sb("got", [P, U, ROW])
        picks, pick = sb("picks", [P, U, 2, 2]), sb("pick", [P, U, 2])
        wgu, wd = sb("wgu", [P, U, 2, 2 * FE]), sb("wd", [FE, U, 2, D])
        xb = sb("xb", [P, 2, P])
        sg, h = sb("sg", [FE, 2, P]), sb("h", [FE, 2, 2, P])
        y = sb("y", [P, U, D])
        FARROW = 65536.0
        ps = k.ps
        w_in, g_in, s_out = sems("w_in"), sems("g_in"), sems("s_out")
        (prep, token_done, tr_done, xb_done, picks_done, pick_done, dest_done, gu_done, silu_done, h_done, yp_done, y_done) = map(
            sem, "prep token_done tr_done xb_done picks_done pick_done dest_done gu_done silu_done h_done yp_done y_done".split())
        block = ctx.enter_context(nc.Block())
        DEPTH = 6
        L_GOT, L_GU, L_Y, L_SC = 3, 4, 5, 6

        @block.sync
        def _(sp):
            def step(kk, u):
                if live(kk, u, 0, PAIRS, U):
                    g, t, r = lagged(kk, u, 0, U)
                    if beyond(t, U):
                        sp.wait_ge(yp_done, t - U + 1)
                    sp.dma_start(wgu[:, r, :, :], a["wgu"][bass.ds(t * P, P), :].rearrange("p (h w) -> p h w", h=2)).then_inc(w_in[r], 16)
                    sp.dma_start(wd[:, r, :, :], a["wd"][bass.ds(t * FE, FE), :].rearrange("p (h w) -> p h w", h=2)).then_inc(w_in[r], 16)
            steps(sp, PAIRS, DEPTH, step, U)

        @block.gpsimd
        def _(pool):
            pool.wait_ge(token_done, 1)
            def step(kk, u):
                if live(kk, u, 0, PAIRS, U):
                    g, t, r = lagged(kk, u, 0, U)
                    if beyond(t, U):
                        pool.wait_ge(tr_done, t - U + 1)
                        pool.wait_ge(picks_done, t - U + 1)
                    pool.indirect_dma_start(got[:, r, :], None, k.rows, bass.IndirectOffsetOnAxis(ap=token[:, t:t + 1], axis=0)).then_inc(g_in[r], 16)
                if live(kk, u, L_SC, PAIRS, U):
                    g, t, r = lagged(kk, u, L_SC, U)
                    pool.wait_ge(dest_done, t + 1)
                    pool.wait_ge(y_done, t + 1)
                    pool.indirect_dma_start(k.contrib, bass.IndirectOffsetOnAxis(ap=dest[:, r, :], axis=0), y[:, r, :], None,
                                            bounds_check=DUMP - 1, oob_is_err=False).then_inc(s_out[r], 16)
            steps(pool, PAIRS, DEPTH, step, U, rolled=False)
            for i in range(U):
                pool.wait_ge(s_out[i], 16 * (PAIRS // U))

        @block.tensor
        def _(pe):
            def step(kk, u):
                if live(kk, u, L_GOT, PAIRS, U):
                    g, t, r = lagged(kk, u, L_GOT, U)
                    pe.wait_ge(g_in[r], g * 16 + 16)
                    if beyond(t, 1):
                        pe.wait_ge(xb_done, t)
                    pe.transpose(ps[0][:, 0:P], got[:, r, 0:D], k.ident[:]).then_inc(tr_done, 1)
                if live(kk, u, L_GU, PAIRS, U):
                    g, t, r = lagged(kk, u, L_GU, U)
                    pe.wait_ge(xb_done, t + 1)
                    pe.wait_ge(w_in[r], g * 32 + 32)
                    if beyond(t, 2):
                        pe.wait_ge(h_done, t - 1)
                    for q in range(2):
                        for e in range(2):
                            mm = pe.matmul(ps[1 + r % 2][0:FE, (2 * q + e) * CAP:(2 * q + e + 1) * CAP], wgu[:, r, e, q * FE:(q + 1) * FE],
                                           xb[:, r % 2, e:P:2], start=True, stop=True)
                    mm.then_inc(gu_done, 1)
                if live(kk, u, L_Y, PAIRS, U):
                    g, t, r = lagged(kk, u, L_Y, U)
                    pe.wait_ge(h_done, t + 1)
                    if beyond(t, 2):
                        pe.wait_ge(y_done, t - 1)
                    for e in range(2):
                        mm = pe.matmul(ps[3 + r % 2][:, 0:D], h[:, r % 2, e, :], wd[:, r, e, :], start=e == 0, stop=e == 1)
                    mm.then_inc(yp_done, 1)
            steps(pe, PAIRS, DEPTH, step, U)

        @block.scalar
        def _(act):
            def step(kk, u):
                if live(kk, u, L_GOT, PAIRS, U):
                    g, t, r = lagged(kk, u, L_GOT, U)
                    act.wait_ge(tr_done, t + 1)
                    if beyond(t, 2):
                        act.wait_ge(gu_done, t - 1)
                    act.activation(xb[:, r % 2, :], ps[0][:, 0:P], ACT.Copy).then_inc(xb_done, 1)
                if live(kk, u, L_GU, PAIRS, U):
                    g, t, r = lagged(kk, u, L_GU, U)
                    act.wait_ge(gu_done, t + 1)
                    if beyond(t, 2):
                        act.wait_ge(h_done, t - 1)
                    act.activation(sg[:, r % 2, :], ps[1 + r % 2][0:FE, 0:P], ACT.Silu).then_inc(silu_done, 1)
                if live(kk, u, L_Y, PAIRS, U):
                    g, t, r = lagged(kk, u, L_Y, U)
                    act.wait_ge(yp_done, t + 1)
                    act.wait_ge(pick_done, t + 1)
                    if beyond(t, U):
                        act.wait_ge(s_out[r], g * 16)
                    act.activation(y[:, r, :], ps[3 + r % 2][:, 0:D], ACT.Copy, scale=pick[:, r, 0:1]).then_inc(y_done, 1)
            steps(act, PAIRS, DEPTH, step, U)

        @block.vector
        def _(dve):
            n = [0]

            def chain(i):
                i.then_inc(prep, 1)
                n[0] += 1
                dve.wait_ge(prep, n[0])
            chain(dve.memset(h[:], 0.0))
            chain(dve.tensor_copy(tab[:].rearrange("p g w -> p (g w)"), ps[7][:, 0:4 * PAIRS]))
            chain(dve.scalar_tensor_tensor(tok[:], tab[:, :, 0], float(TILE), tab[:, :, 1], ALU.mult, ALU.add))
            dve.tensor_copy(token[:], tok[:]).then_inc(token_done, 1)
            chain(dve.tensor_scalar(tok8[:], tok[:], float(TOPK), -1.0, ALU.mult, ALU.add))
            chain(dve.tensor_scalar(none[:], tab[:, :, 2], -FARROW, FARROW, ALU.mult, ALU.add))
            chain(dve.tensor_tensor(tok8[:], tok8[:], none[:], ALU.add))
            chain(dve.scalar_tensor_tensor(dest0[:], tab[:, :, 3], -float(TOPK), tok8[:], ALU.mult, ALU.add))

            def step(kk, u):
                if live(kk, u, L_GOT, PAIRS, U):
                    g, t, r = lagged(kk, u, L_GOT, U)
                    dve.wait_ge(g_in[r], g * 16 + 16)
                    if beyond(t, U):
                        dve.wait_ge(pick_done, t - U + 1)
                    wr = got[:, r, D:ROW].rearrange("p (q e) -> p q e", q=2)[:, :, bass.ds(t * 2, 2)]
                    dve.tensor_tensor(picks[:, r, :, :], wr, k.parmask[:].unsqueeze(1).to_broadcast([P, 2, 2]), ALU.mult).then_inc(picks_done, 1)
                    if beyond(t, U):
                        dve.wait_ge(y_done, t - U + 1)
                    dve.wait_ge(picks_done, t + 1)
                    dve.tensor_reduce(pick[:, r, :], picks[:, r, :, :], AX.X, ALU.add).then_inc(pick_done, 1)
                    if beyond(t, U):
                        dve.wait_ge(s_out[r], g * 16)
                    dve.wait_ge(pick_done, t + 1)
                    dve.tensor_tensor(dest[:, r, :], pick[:, r, 1:2], dest0[:, bass.ds(t, 1)], ALU.add).then_inc(dest_done, 1)
                if live(kk, u, L_GU, PAIRS, U):
                    g, t, r = lagged(kk, u, L_GU, U)
                    dve.wait_ge(silu_done, t + 1)
                    if beyond(t, 2):
                        dve.wait_ge(yp_done, t - 1)
                    for e in range(2):
                        cols = slice(e * CAP, (e + 1) * CAP)
                        i = dve.tensor_tensor(h[:, r % 2, e, e:P:2], sg[:, r % 2, cols], ps[1 + r % 2][0:FE, P + e * CAP:P + (e + 1) * CAP], ALU.mult)
                    i.then_inc(h_done, 1)
            steps(dve, PAIRS, DEPTH, step, U)


def stage_d_sum(nc, k, a):
    U = 4
    with ExitStack() as ctx:
        sb = lambda n, s, t=F32: ctx.enter_context(nc.sbuf_tensor("f_" + n, s, t))
        sem = cleared_later(nc, ctx, "f_")
        sems = lambda n: [sem(f"{n}{i}") for i in range(U)]
        st, mv, var, rstd, mark = sb("st", [P, 2, 6]), sb("mv", [P, 4, 2]), sb("var", [P, 2, 1]), sb("rstd", [P, 4, 1]), sb("mark", [P, 1])
        con, out = sb("con", [P, U, TOPK, D]), sb("out", [P, U, D])
        c_in, o_out = sems("c_in"), sems("o_out")
        clean = sem("clean")
        (sum_done, st_done, mv_done, var_done, rstd_done, out_done) = map(
            sem, "sum_done st_done mv_done var_done rstd_done out_done".split())
        total = k.ps[0:U]
        block = ctx.enter_context(nc.Block())
        DEPTH = 4
        L_SUM, L_STAT, L_OUT = 1, 2, 3
        contrib = k.contrib.rearrange("(t r) d -> t (r d)", r=TOPK)

        @block.sync
        def _(sp):
            def step(kk, u):
                if live(kk, u, 0, NT, U):
                    g, t, r = lagged(kk, u, 0, U)
                    if beyond(t, U):
                        sp.wait_ge(sum_done, t - U + 1)
                    sp.dma_start(con[:, r, :, :].rearrange("p r d -> p (r d)"), contrib[bass.ds(t * P, P), :]).then_inc(c_in[r], 16)
            steps(sp, NT, DEPTH, step, U)

        @block.tensor
        def _(pe):
            def step(kk, u):
                if live(kk, u, L_SUM, NT, U):
                    g, t, r = lagged(kk, u, L_SUM, U)
                    if beyond(t, U):
                        pe.wait_ge(out_done, t - U + 1)
                    pe.wait_ge(c_in[r], g * 16 + 16)
                    for i in range(TOPK):
                        pe.matmul(total[r][:, 0:D], k.ident[:], con[:, r, i, :], start=i == 0, stop=False)
                    pe.matmul(total[r][:, 0:D], k.ident[:], k.base[:, bass.ds(t, 1), :].rearrange("p o d -> p (o d)"),
                              start=False, stop=True).then_inc(sum_done, 1)
            steps(pe, NT, DEPTH, step, U)

        @block.scalar
        def _(act):
            def step(kk, u):
                if live(kk, u, L_OUT, NT, U):
                    g, t, r = lagged(kk, u, L_OUT, U)
                    act.wait_ge(out_done, t + 1)
                    act.dma_start(a["out"][bass.ds(t * P, P), :], out[:, r, :]).then_inc(o_out[r], 16)
            steps(act, NT, DEPTH, step, U)
            for i in range(U):
                act.wait_ge(o_out[i], 16 * (NT // U))

        @block.vector
        def _(dve):
            dve.memset(mv[:], 0.0).then_inc(clean, 1)
            dve.wait_ge(clean, 1)

            def step(kk, u):
                if live(kk, u, L_STAT, NT, U):
                    g, t, r = lagged(kk, u, L_STAT, U)
                    dve.wait_ge(sum_done, t + 1)
                    if beyond(t, 2):
                        dve.wait_ge(mv_done, t - 1)
                    dve.bn_stats(st[:, r % 2, :], total[r][:, 0:D]).then_inc(st_done, 1)
                if live(kk, u, L_OUT, NT, U):
                    g, t, r = lagged(kk, u, L_OUT, U)
                    dve.wait_ge(rstd_done, t + 1)
                    if beyond(t, U):
                        dve.wait_ge(o_out[r], g * 16)
                    dve.tensor_scalar(out[:, r, :], total[r][:, 0:D], mv[:, r, 0:1], rstd[:, r, :], ALU.subtract, ALU.mult).then_inc(out_done, 1)
                if live(kk, u, L_STAT, NT, U):
                    g, t, r = lagged(kk, u, L_STAT, U)
                    dve.wait_ge(st_done, t + 1)
                    dve.tensor_copy(mark[:], st[:, r % 2, 0:1])
                    dve.bn_aggr(mv[:, r, :], st[:, r % 2, :]).then_inc(mv_done, 1)
            steps(dve, NT, DEPTH, step, U)

        @block.gpsimd
        def _(pool):
            def step(kk, u):
                if live(kk, u, L_STAT, NT, U):
                    g, t, r = lagged(kk, u, L_STAT, U)
                    pool.wait_ge(mv_done, t + 1)
                    if beyond(t, 2):
                        pool.wait_ge(rstd_done, t - 1)
                    pool.tensor_tensor(var[:, r % 2, :], mv[:, r, 1:2], k.eps5[:, 0:1], ALU.add).then_inc(var_done, 1)
                    if beyond(t, U):
                        pool.wait_ge(out_done, t - U + 1)
                    pool.wait_ge(var_done, t + 1)
                    pool.tensor_tensor(rstd[:, r, :], var[:, r % 2, :], k.mhalf[:, 0:1], ALU.pow).then_inc(rstd_done, 1)
            steps(pool, NT, DEPTH, step, U)


def build(nc, a):
    with ExitStack() as ctx:
        k = Shared(nc, ctx)
        constants(nc, k, a)
        stage_a(nc, k, a)
        stage_b(nc, k, a)
        stage_c(nc, k, a)
        stage_d_route(nc, k, a)
        stage_d_experts(nc, k, a)
        stage_d_sum(nc, k, a)


def layout(x):
    import numpy as np
    c = np.ascontiguousarray
    t = lambda w: np.swapaxes(w, -1, -2)
    x = {n: np.asarray(v) for n, v in x.items()}
    tok = x["L0_attn_x"].reshape(TOKENS, D)
    out = {
        "x": c(tok), "xt": c(tok.T),
        "wqkv": c(np.concatenate([x["L0_attn_Wq"].T, x["L0_attn_Wk"].T, x["L0_attn_Wv"].T], 1)),
        "wfc": c(x["L0_attn_Wfc"].T),
    }
    out["wffn"] = c(np.concatenate([x["L0_ffn_w_gate"].T, x["L0_ffn_w_up"].T]
                    + [x["L0_ffn_w_down"][:, j * P:(j + 1) * P].T for j in range(NJ)], 1))
    v = {n[8:]: w for n, w in x.items() if n.startswith("L1_attn_")}
    col = lambda n: v[n][:, :, None]
    out["w1"] = c(np.concatenate([v["Wq"], v["Wk"], v["Wv"], col("bq"), col("bk"), col("bv")], 2).reshape(BLOCKS * P, W1COLS))
    w2r = v["W2"].reshape(BLOCKS, NF, P, D).transpose(0, 2, 1, 3).reshape(BLOCKS, P, NF * D)
    b1r = v["b1"].reshape(BLOCKS, NF, P).transpose(0, 2, 1)
    out["w2"] = c(np.concatenate([v["Wo"], col("bo"), col("ln1_s"), col("ln1_b"), v["W1"], b1r, w2r, col("b2"),
                                  col("ln2_s"), col("ln2_b")], 2).reshape(BLOCKS * P, W2COLS))
    f = {n[7:]: w for n, w in x.items() if n.startswith("L1_ffn_")}
    out["ws"] = c(np.concatenate([f["router_w"].T, f["ws_gate_up"]], 1))
    out["wsd"] = c(f["ws_down"])
    pair = lambda w, m: w.reshape(PAIRS, 2, m, -1).transpose(0, 2, 1, 3).reshape(PAIRS * m, -1)
    out["wgu"] = c(pair(np.concatenate([f["w_gate"], f["w_up"]], 2), D))
    out["wd"] = c(pair(f["w_down"], FE))
    return out


def kernel(**inputs):
    import concourse.bacc as bacc
    import numpy as np
    from concourse.bass_utils import run_bass_kernel_spmd

    nc = bacc.Bacc("TRN2", target_bir_lowering=False, num_devices=1)
    arrays = layout(inputs)
    a = {n: nc.dram_tensor("in_" + n, v.shape, mybir.dt.from_np(v.dtype), kind="ExternalInput").ap() for n, v in arrays.items()}
    a["out"] = nc.dram_tensor("out_0", [TOKENS, D], F32, kind="ExternalOutput").ap()
    build(nc, a)
    r = run_bass_kernel_spmd(nc, [{"in_" + n: v for n, v in arrays.items()}], core_ids=[0])
    return np.asarray(r.results[0]["out_0"]).reshape(8, CH, D)
```
